# Optimizing a Trainium2 kernel written in Bass

```python
import numpy as np
import jax
import jax.numpy as jnp

def _softmax(x, axis=-1):
    return jax.nn.softmax(x, axis=axis)

def _gelu(x):
    return jax.nn.gelu(x, approximate=True)

def _silu(x):
    return jax.nn.silu(x)

def _sigmoid(x):
    return jax.nn.sigmoid(x)

def _layernorm(x, axis=-1, eps=1e-05):
    m = jnp.mean(x, axis=axis, keepdims=True)
    v = jnp.var(x, axis=axis, keepdims=True)
    return (x - m) / jnp.sqrt(v + eps)

def _scatter_add(tgt, idx, src, axis=0):
    return tgt.at[idx].add(src)

def _segment_sum(src, seg, n):
    return jax.ops.segment_sum(src, seg, n)
kernel_name = 'mk_adaln_attn_ffn_d1_seqx_r8_e07daf'

def setup_inputs(seed: int=0):
    np.random.seed(seed)
    _w = jnp.asarray

    def _rec_inputs():
        import jax
        import jax.numpy as jnp
        _rk = jax.random.key(seed)
        x = -1.394e-06 + 0.9999 * jax.random.normal(jax.random.fold_in(_rk, 1), (32, 32, 256), jnp.float32)
        _lenS = 32 - jax.random.randint(jax.random.fold_in(_rk, 7), (32,), 0, max(1, 32 // 4) + 1, jnp.int32)
        _lenS2 = 32 - jax.random.randint(jax.random.fold_in(_rk, 8), (32,), 0, max(1, 32 // 4) + 1, jnp.int32)
        cond_2048 = -0.00499425 + 1.0058 * jax.random.normal(jax.random.fold_in(_rk, 11), (32, 256), jnp.float32)
        return (x, cond_2048)
    x, cond_2048 = _rec_inputs()

    def _L0_cond_setup():
        import jax, jax.numpy as jnp
        import numpy as np
        B, T, D = (16, 128, 256)
        key = jax.random.key(seed)
        k0, k1, k2, k3 = jax.random.split(key, 4)
        scale = 1.0 / np.sqrt(D)
        return {'initial_state': jax.random.normal(k0, (B, D), jnp.float32), 'inputs': jax.random.normal(k1, (B, T, D), jnp.float32), 'W_ih': jax.random.normal(k2, (D, 3 * D), jnp.float32) * scale, 'W_hh': jax.random.normal(k3, (D, 3 * D), jnp.float32) * scale, 'b_ih': jnp.zeros((3 * D,), jnp.float32), 'b_hh': jnp.zeros((3 * D,), jnp.float32)}
    _L0_cond_all = _L0_cond_setup()
    _L0_cond_in = {k: v for k, v in _L0_cond_all.items() if k in ('W_ih', 'W_hh', 'b_ih', 'b_hh')}
    del _L0_cond_all

    def _L0_attn_setup():
        import jax, jax.numpy as jnp
        import numpy as np
        import math
        HIDDEN = 256
        NUM_HEADS = 32
        HEAD_DIM = 64
        WINDOW = 128
        GLOBAL_HEADS = 2
        LOCAL_HEADS = NUM_HEADS - GLOBAL_HEADS
        ROPE_BASE = 10000.0

        def rotate_half(x):
            x1, x2 = jnp.split(x, 2, axis=-1)
            return jnp.concatenate([-x2, x1], axis=-1)

        def rope_cos_sin(positions, dim):
            inv_freq = 1.0 / ROPE_BASE ** (jnp.arange(0, dim, 2, dtype=jnp.float32) / dim)
            freqs = positions[:, None].astype(jnp.float32) * inv_freq[None, :]
            emb = jnp.concatenate([freqs, freqs], axis=-1)
            return (jnp.cos(emb)[None, None], jnp.sin(emb)[None, None])

        def apply_rope(q, k, q_pos, k_pos):
            cos_q, sin_q = rope_cos_sin(q_pos, q.shape[-1])
            cos_k, sin_k = rope_cos_sin(k_pos, k.shape[-1])
            return (q * cos_q + rotate_half(q) * sin_q, k * cos_k + rotate_half(k) * sin_k)

        def sliding_window_attention_blockwise(q, k, v, window_size):
            B, H, L, D = q.shape
            block = min(window_size, 128)
            scale = 1.0 / math.sqrt(D)
            outs = []
            for start in range(0, L, block):
                end = min(start + block, L)
                ks = max(0, start - window_size // 2)
                ke = end
                qb = q[:, :, start:end]
                kb = k[:, :, ks:ke]
                vb = v[:, :, ks:ke]
                s = jnp.einsum('bhqd,bhkd->bhqk', qb, kb) * scale
                qi = jnp.arange(start, end)[:, None]
                ki = jnp.arange(ks, ke)[None, :]
                s = jnp.where(qi >= ki, s, -jnp.inf)
                a = jax.nn.softmax(s, axis=-1)
                outs.append(jnp.einsum('bhqk,bhkd->bhqd', a, vb))
            return jnp.concatenate(outs, axis=2)

        def global_attention(q, k, v):
            B, H, L, D = q.shape
            scale = 1.0 / math.sqrt(D)
            s = jnp.einsum('bhqd,bhkd->bhqk', q, k) * scale
            causal = jnp.tril(jnp.ones((L, L), dtype=bool))
            s = jnp.where(causal[None, None], s, -jnp.inf)
            a = jax.nn.softmax(s, axis=-1)
            return jnp.einsum('bhqk,bhkd->bhqd', a, v)
        key = jax.random.key(seed)
        k1, k2, k3, k4, k5, k6 = jax.random.split(key, 6)
        B, L = (2, 512)
        P = NUM_HEADS * HEAD_DIM
        return {'hidden_states': jax.random.normal(k1, (B, L, HIDDEN), dtype=jnp.float32), 'Wq': jax.random.normal(k2, (P, HIDDEN), dtype=jnp.float32) * 0.02, 'Wk': jax.random.normal(k3, (P, HIDDEN), dtype=jnp.float32) * 0.02, 'Wv': jax.random.normal(k4, (P, HIDDEN), dtype=jnp.float32) * 0.02, 'Wo': jax.random.normal(k5, (HIDDEN, P), dtype=jnp.float32) * 0.02, 'bo': jax.random.normal(k6, (HIDDEN,), dtype=jnp.float32) * 0.02}
    _L0_attn_all = _L0_attn_setup()
    _L0_attn_in = {k: v for k, v in _L0_attn_all.items() if k in ('Wq', 'Wk', 'Wv', 'Wo', 'bo')}
    del _L0_attn_all

    def _L0_cond2_setup():
        import jax, jax.numpy as jnp
        import numpy as np
        key = jax.random.key(seed)
        k1, k2, k3 = jax.random.split(key, 3)
        B, L, D, K = (4, 512, 256, 4)
        x = jax.random.normal(k1, (B, L, D), dtype=jnp.float32)
        w = jax.random.normal(k2, (K, 1, D), dtype=jnp.float32) * 0.1
        b = jax.random.normal(k3, (D,), dtype=jnp.float32) * 0.1
        return {'x': x, 'w': w, 'b': b}
    _L0_cond2_all = _L0_cond2_setup()
    _L0_cond2_in = {k: v for k, v in _L0_cond2_all.items() if k in ('b',)}
    del _L0_cond2_all

    def _L0_ffn_setup():
        import jax, jax.numpy as jnp
        import numpy as np
        N_EXPERTS = 8
        TOP_K = 2
        D_MODEL = 256
        D_FF = 128
        BATCH, SEQ = (2, 256)

        def _trunc_normal(key, shape, fan_in):
            std = jnp.sqrt(1.0 / 3.0) / jnp.sqrt(float(fan_in))
            return jax.random.truncated_normal(key, -2.0, 2.0, shape, dtype=jnp.float32) * std
        key = jax.random.key(seed)
        kx, kr, k1, k2, k3 = jax.random.split(key, 5)
        x = jax.random.normal(kx, (BATCH, SEQ, D_MODEL), dtype=jnp.float32)
        router_w = jax.random.uniform(kr, (N_EXPERTS, D_MODEL), dtype=jnp.float32, minval=-1.0, maxval=1.0) / jnp.sqrt(float(D_MODEL))
        w1 = _trunc_normal(k1, (N_EXPERTS, D_MODEL, D_FF), D_MODEL)
        w2 = _trunc_normal(k2, (N_EXPERTS, D_MODEL, D_FF), D_MODEL)
        w3 = _trunc_normal(k3, (N_EXPERTS, D_FF, D_MODEL), D_FF)
        return {'x': x, 'router_w': router_w, 'w1': w1, 'w2': w2, 'w3': w3}
    _L0_ffn_all = _L0_ffn_setup()
    _L0_ffn_in = {k: v for k, v in _L0_ffn_all.items() if k in ('router_w', 'w1', 'w2', 'w3')}
    del _L0_ffn_all
    return {'x': x, 'cond_2048': cond_2048, 'L0_cond_W_ih': _L0_cond_in['W_ih'], 'L0_cond_W_hh': _L0_cond_in['W_hh'], 'L0_cond_b_ih': _L0_cond_in['b_ih'], 'L0_cond_b_hh': _L0_cond_in['b_hh'], 'L0_attn_Wq': _L0_attn_in['Wq'], 'L0_attn_Wk': _L0_attn_in['Wk'], 'L0_attn_Wv': _L0_attn_in['Wv'], 'L0_attn_Wo': _L0_attn_in['Wo'], 'L0_attn_bo': _L0_attn_in['bo'], 'L0_cond2_b': _L0_cond2_in['b'], 'L0_ffn_router_w': _L0_ffn_in['router_w'], 'L0_ffn_w1': _L0_ffn_in['w1'], 'L0_ffn_w2': _L0_ffn_in['w2'], 'L0_ffn_w3': _L0_ffn_in['w3']}

def reference(x, cond_2048, L0_cond_W_ih, L0_cond_W_hh, L0_cond_b_ih, L0_cond_b_hh, L0_attn_Wq, L0_attn_Wk, L0_attn_Wv, L0_attn_Wo, L0_attn_bo, L0_cond2_b, L0_ffn_router_w, L0_ffn_w1, L0_ffn_w2, L0_ffn_w3):
    import jax
    import jax.numpy as jnp

    def _L0_cond_ref(initial_state, inputs, W_ih, W_hh, b_ih, b_hh):
        import jax, jax.numpy as jnp
        import numpy as np
        B, T, D = (16, 128, 256)
        "ScanOverTime(GRU cell): sequential per-timestep module call with\n            dict-state passing; merge_dict_trees stacks the per-step\n            'state_predicted' tensors along axis=1 -> [B, T, D]."

        def cell(h, x):
            gi = x @ W_ih + b_ih
            gh = h @ W_hh + b_hh
            i_r, i_z, i_n = jnp.split(gi, 3, axis=-1)
            h_r, h_z, h_n = jnp.split(gh, 3, axis=-1)
            r = jax.nn.sigmoid(i_r + h_r)
            z = jax.nn.sigmoid(i_z + h_z)
            n = jnp.tanh(i_n + r * h_n)
            h_new = (1.0 - z) * n + z * h
            return (h_new, h_new)
        xs = jnp.swapaxes(inputs, 0, 1)
        _, hs = jax.lax.scan(cell, initial_state, xs)
        return jnp.swapaxes(hs, 0, 1)

    def _L0_attn_ref(hidden_states, Wq, Wk, Wv, Wo, bo):
        import jax, jax.numpy as jnp
        import numpy as np
        import math
        HIDDEN = 256
        NUM_HEADS = 32
        HEAD_DIM = 64
        WINDOW = 128
        GLOBAL_HEADS = 2
        LOCAL_HEADS = NUM_HEADS - GLOBAL_HEADS
        ROPE_BASE = 10000.0

        def rotate_half(x):
            x1, x2 = jnp.split(x, 2, axis=-1)
            return jnp.concatenate([-x2, x1], axis=-1)

        def rope_cos_sin(positions, dim):
            inv_freq = 1.0 / ROPE_BASE ** (jnp.arange(0, dim, 2, dtype=jnp.float32) / dim)
            freqs = positions[:, None].astype(jnp.float32) * inv_freq[None, :]
            emb = jnp.concatenate([freqs, freqs], axis=-1)
            return (jnp.cos(emb)[None, None], jnp.sin(emb)[None, None])

        def apply_rope(q, k, q_pos, k_pos):
            cos_q, sin_q = rope_cos_sin(q_pos, q.shape[-1])
            cos_k, sin_k = rope_cos_sin(k_pos, k.shape[-1])
            return (q * cos_q + rotate_half(q) * sin_q, k * cos_k + rotate_half(k) * sin_k)

        def sliding_window_attention_blockwise(q, k, v, window_size):
            B, H, L, D = q.shape
            block = min(window_size, 128)
            scale = 1.0 / math.sqrt(D)
            outs = []
            for start in range(0, L, block):
                end = min(start + block, L)
                ks = max(0, start - window_size // 2)
                ke = end
                qb = q[:, :, start:end]
                kb = k[:, :, ks:ke]
                vb = v[:, :, ks:ke]
                s = jnp.einsum('bhqd,bhkd->bhqk', qb, kb) * scale
                qi = jnp.arange(start, end)[:, None]
                ki = jnp.arange(ks, ke)[None, :]
                s = jnp.where(qi >= ki, s, -jnp.inf)
                a = jax.nn.softmax(s, axis=-1)
                outs.append(jnp.einsum('bhqk,bhkd->bhqd', a, vb))
            return jnp.concatenate(outs, axis=2)

        def global_attention(q, k, v):
            B, H, L, D = q.shape
            scale = 1.0 / math.sqrt(D)
            s = jnp.einsum('bhqd,bhkd->bhqk', q, k) * scale
            causal = jnp.tril(jnp.ones((L, L), dtype=bool))
            s = jnp.where(causal[None, None], s, -jnp.inf)
            a = jax.nn.softmax(s, axis=-1)
            return jnp.einsum('bhqk,bhkd->bhqd', a, v)
        B, L, _ = hidden_states.shape
        q = jnp.einsum('blh,ph->blp', hidden_states, Wq).reshape(B, L, NUM_HEADS, HEAD_DIM).transpose(0, 2, 1, 3)
        k = jnp.einsum('blh,ph->blp', hidden_states, Wk).reshape(B, L, NUM_HEADS, HEAD_DIM).transpose(0, 2, 1, 3)
        v = jnp.einsum('blh,ph->blp', hidden_states, Wv).reshape(B, L, NUM_HEADS, HEAD_DIM).transpose(0, 2, 1, 3)
        pos = jnp.arange(L)
        q, k = apply_rope(q, k, pos, pos)
        ql, qg = (q[:, :LOCAL_HEADS], q[:, LOCAL_HEADS:])
        kl, kg = (k[:, :LOCAL_HEADS], k[:, LOCAL_HEADS:])
        vl, vg = (v[:, :LOCAL_HEADS], v[:, LOCAL_HEADS:])
        out_local = sliding_window_attention_blockwise(ql, kl, vl, WINDOW)
        out_global = global_attention(qg, kg, vg)
        out = jnp.concatenate([out_local, out_global], axis=1)
        out = out.transpose(0, 2, 1, 3).reshape(B, L, NUM_HEADS * HEAD_DIM)
        return jnp.einsum('blp,hp->blh', out, Wo) + bo

    def _L0_cond2_ref(x, w, b):
        import jax, jax.numpy as jnp
        import numpy as np
        'Depthwise causal conv1d, channel-last.\n            x: (B, L, D); w: (K, 1, D); b: (D,). Returns (B, L, D).\n            Matches torch: Conv1d(D, D, K, groups=D, padding=K-1)(x.T)[..., :L].T\n            which is exactly a causal conv (left pad K-1, trim to L).\n            '
        K = w.shape[0]
        D = x.shape[-1]
        y = jax.lax.conv_general_dilated(x, w, window_strides=(1,), padding=[(K - 1, 0)], feature_group_count=D, dimension_numbers=('NWC', 'WIO', 'NWC'))
        return y + b

    def _L0_ffn_ref(x, router_w, w1, w2, w3):
        import jax, jax.numpy as jnp
        import numpy as np
        N_EXPERTS = 8
        TOP_K = 2
        D_MODEL = 256
        D_FF = 128
        BATCH, SEQ = (2, 256)

        def _trunc_normal(key, shape, fan_in):
            std = jnp.sqrt(1.0 / 3.0) / jnp.sqrt(float(fan_in))
            return jax.random.truncated_normal(key, -2.0, 2.0, shape, dtype=jnp.float32) * std
        B, S, D = x.shape
        xf = x.reshape(-1, D)
        n_tokens = xf.shape[0]
        logits = xf @ router_w.T
        topk_vals, topk_idx = jax.lax.top_k(logits, TOP_K)
        topk_weights = jax.nn.softmax(topk_vals, axis=-1)
        gate = jax.nn.silu(jnp.einsum('nd,edf->enf', xf, w1))
        value = jnp.einsum('nd,edf->enf', xf, w2)
        expert_out = jnp.einsum('enf,efd->end', gate * value, w3)
        tok = jnp.arange(n_tokens)[:, None]
        selected = expert_out[topk_idx, tok]
        out = jnp.sum(selected * topk_weights[..., None], axis=1)
        return out.reshape(B, S, D)
    x = x + _L0_attn_ref(_L0_cond_ref(cond_2048, x, L0_cond_W_ih, L0_cond_W_hh, L0_cond_b_ih, L0_cond_b_hh), L0_attn_Wq, L0_attn_Wk, L0_attn_Wv, L0_attn_Wo, L0_attn_bo)
    x = x + _L0_ffn_ref(_L0_cond2_ref(x, cond_2048[:, None, :], L0_cond2_b), L0_ffn_router_w, L0_ffn_w1, L0_ffn_w2, L0_ffn_w3)
    return x

_drawn_inputs = setup_inputs


def setup_inputs(seed=0):
    import zlib

    import numpy as np

    out = dict(_drawn_inputs(seed))
    spreads = {'L0_cond_b_ih': (0.0, 0.1), 'L0_cond_b_hh': (0.0, 0.1)}
    factors = {'L0_attn_Wq': 3.404, 'L0_attn_Wk': 3.506}
    for name, (base, spread) in spreads.items():
        noise = np.random.default_rng([zlib.crc32(name.encode()), seed]).standard_normal(out[name].shape)
        drawn = base * np.exp(spread * noise) if base else spread * noise
        out[name] = jnp.asarray(drawn.astype(out[name].dtype))
    for name, factor in factors.items():
        out[name] = (out[name] * factor).astype(out[name].dtype)
    return out
```

```python
from contextlib import ExitStack

import concourse.bass as bass
from concourse import mybir

F32 = mybir.dt.float32
F16 = mybir.dt.float16
U32 = mybir.dt.uint32
ALU = mybir.AluOpType
ACT = mybir.ActivationFunctionType
AX = mybir.AxisListType

P = 128
BATCH, STEPS, DIM = 32, 32, 256
TOKENS = BATCH * STEPS
KC = DIM // P
HEADS, HEAD_DIM = 32, 64
HALF = HEAD_DIM // 2
PER_GROUP = P // HALF
GROUPS = HEADS // PER_GROUP
CB = 4
CW = DIM // CB
TILE_B = P // STEPS
TILES = TOKENS // P
BH = BATCH // 2
TH = TOKENS // 2
TILES_H = TILES // 2
HP = PER_GROUP // 2
VW = PER_GROUP * HEAD_DIM
EXPERTS, FF = 8, 128
TAPS = STEPS
QUARTERS = 4
QB = BATCH // QUARTERS
QT = TOKENS // QUARTERS
QTILES = QT // P
SPLIT = 256.0

QKV_COLS = KC * 3 * DIM
WO_COLS = HP * DIM
W1_COLS = EXPERTS * KC * FF
W3_COLS = EXPERTS * DIM
RW_COLS = KC * EXPERTS
W1_AT, W2_AT, W3_AT = 0, W1_COLS, 2 * W1_COLS
QKV_AT = W3_AT + W3_COLS
WO_AT = QKV_AT + QKV_COLS
RW_AT = WO_AT + WO_COLS
SPLIT_COLS = RW_AT + RW_COLS
A_LOOPS = STEPS // 2
SPLIT_STEP = SPLIT_COLS // A_LOOPS
assert SPLIT_STEP * A_LOOPS == SPLIT_COLS

ROT = 6
TAB_MASK = ROT * STEPS
TAB_IDENT = TAB_MASK + STEPS
TAB_IOTA = TAB_IDENT + P
TAB_COLS = TAB_IOTA + EXPERTS


def block_kernel(nc: bass.Bass, x_t, h0, w_ih, w_hh, gate_bias, w_first, w_qkv, w_o, bo, tables, taps, conv_b, out):
    ctx = ExitStack()
    with ctx:
        def sb(name, shape, dt=F32):
            return ctx.enter_context(nc.sbuf_tensor(name, shape, dt))

        def pb(name, shape):
            return ctx.enter_context(nc.psum_tensor(name, shape, F32))

        def sem(name):
            return ctx.enter_context(nc.semaphore(name))

        ps_s = pb("ps_s", [P, 2, 512])
        ps_qk = pb("ps_qk", [P, 4, 512])
        ps_o = pb("ps_o", [P, 2, 512])

        xT = sb("xT", [P, KC, STEPS + 2, BATCH])
        x2 = sb("x2", [P, KC, BATCH, STEPS])
        hs_hi = sb("hs_hi", [P, KC, BATCH, STEPS], F16)
        hs_lo = sb("hs_lo", [P, KC, BATCH, STEPS], F16)
        wih = sb("wih", [P, KC, CB, 3 * CW])
        whh = sb("whh", [P, KC, CB, 3 * CW])
        bias_raw = sb("bias_raw", [P, CB, 4 * CW])
        bias16 = sb("bias16", [P, CB, 4 * CW], F16)
        ones16 = sb("ones16", [P, BATCH], F16)
        x_now = sb("x_now", [P, 2, KC, BATCH])
        state = sb("state", [P, CW])
        stateT = sb("stateT", [P, 2, KC, BATCH])
        rz = sb("rz", [P, 2 * CW])
        cand = sb("cand", [P, 3, CW])
        blend = sb("blend", [P, 4, CW])
        arena = sb("arena", [P, SPLIT_COLS])
        w_hi = sb("w_hi", [P, SPLIT_COLS], F16)
        w_lo = sb("w_lo", [P, SPLIT_COLS], F16)
        split_by = sb("split_by", [P, 1])
        raw_qkv = sb("raw_qkv", [P, QKV_COLS])
        raw_o = sb("raw_o", [P, WO_COLS])
        tab = sb("tab", [P, TAB_COLS])
        bo_s = sb("bo_s", [P, KC])
        taps_s = sb("taps_s", [P, KC, TAPS])
        conv_bs = sb("conv_bs", [P, KC])
        k_bd = sb("k_bd", [P, 2, BATCH, PER_GROUP, STEPS])
        v_s = sb("v_s", [P, TILES, VW])
        soft = sb("soft", [P, 2, TILES_H * PER_GROUP, STEPS])
        prob = sb("prob", [P, 2, TILES_H * PER_GROUP, STEPS])
        stats = sb("stats", [P, 2, 3, TILES_H * PER_GROUP])
        p_bd = sb("p_bd", [P, 2, TILES_H * PER_GROUP, P])
        o_hi = sb("o_hi", [P, HP, TOKENS], F16)
        o_lo = sb("o_lo", [P, HP, TOKENS], F16)

        qk_cols = 2 * TOKENS
        q_s = arena[:, 0:qk_cols].rearrange("p (a b t) -> p a b t", a=2, b=BATCH)
        k_s = arena[:, qk_cols:2 * qk_cols].rearrange("p (a b t) -> p a b t", a=2, b=BATCH)
        prods = arena[:, 2 * qk_cols:4 * qk_cols].rearrange("p (u n c) -> p u n c", u=2, n=2)
        c_f = k_bd[:, :, :, :, :].rearrange("p a b h t -> p (a b h t)")
        x2_q = c_f[:, 0:KC * QT].rearrange("p (m c) -> p m c", m=KC)
        y_f = c_f[:, 512:512 + KC * QT].rearrange("p (m b t) -> p m b t", m=KC, b=QB)
        gate_f = c_f[:, 1024:1536].rearrange("p (u c) -> p u c", u=2)
        hid_f = c_f[:, 1536:2048].rearrange("p (u c) -> p u c", u=2)
        out_f = c_f[:, 2048:2560].rearrange("p (q c) -> p q c", q=QTILES)
        y_hi = sb("y_hi", [P, KC, QT], F16)
        y_lo = sb("y_lo", [P, KC, QT], F16)
        hid_hi = sb("hid_hi", [P, 2, QT], F16)
        hid_lo = sb("hid_lo", [P, 2, QT], F16)
        logits = sb("logits", [P, QTILES, EXPERTS])
        top = sb("top", [P, QTILES, 8])
        top_at = sb("top_at", [P, QTILES, 8], U32)
        top_f = sb("top_f", [P, QTILES, 8])
        route = sb("route", [P, QTILES, 4])
        pick = sb("pick", [P, QTILES, 3, EXPERTS])

        rot = [tab[:, n * STEPS:(n + 1) * STEPS] for n in range(ROT)]
        mask = tab[:, TAB_MASK:TAB_MASK + STEPS]
        ident = tab[:, TAB_IDENT:TAB_IDENT + P]
        iota = tab[:, TAB_IOTA:TAB_IOTA + EXPERTS]

        def qkv_w(w, kind, k):
            a = QKV_AT + (k * 3 + kind) * DIM
            return w[:, a:a + DIM]

        def over(table, n):
            return table.rearrange("p (o t) -> p o t", o=1).broadcast_to([P, n, STEPS])

        gru_loaded = sem("gru_loaded")
        bias_loaded = sem("bias_loaded")
        first_loaded = sem("first_loaded")
        consts_loaded = sem("consts_loaded")
        qkv_loaded = sem("qkv_loaded")
        o_loaded = sem("o_loaded")
        bias_zeroed = sem("bias_zeroed")
        bias_ready = sem("bias_ready")
        k_diag_zeroed = sem("k_diag_zeroed")
        pool_set = sem("pool_set")
        x_ready = sem("x_ready")
        x_projected = sem("x_projected")
        gates_ready = sem("gates_ready")
        rz_ready = sem("rz_ready")
        reset_done = sem("reset_done")
        cand_summed = sem("cand_summed")
        cand_ready = sem("cand_ready")
        z_ready = sem("z_ready")
        blend_ready = sem("blend_ready")
        state_new = sem("state_new")
        state_ready = sem("state_ready")
        hs_hi_saved = sem("hs_hi_saved")
        hs_saved = sem("hs_saved")
        w_scaled = sem("w_scaled")
        w_headed = sem("w_headed")
        w_split = sem("w_split")
        x2_updated = sem("x2_updated")
        qk_projected = sem("qk_projected")
        qk_products = sem("qk_products")
        qk_rotated = sem("qk_rotated")
        k_spread = sem("k_spread")
        qk_w_ready = sem("qk_w_ready")
        v_w_ready = sem("v_w_ready")
        o_w_ready = sem("o_w_ready")
        v_projected = sem("v_projected")
        v_ready = sem("v_ready")
        scored = sem("scored")
        masked = sem("masked")
        max_ready = sem("max_ready")
        shifted = sem("shifted")
        exp_ready = sem("exp_ready")
        sum_ready = sem("sum_ready")
        rsum_ready = sem("rsum_ready")
        prob_ready = sem("prob_ready")
        prob_turned = sem("prob_turned")
        attended = sem("attended")
        o_headed = sem("o_headed")
        o_split = sem("o_split")
        o_projected = sem("o_projected")
        quarter_copied = sem("quarter_copied")
        conv_step = [sem(f"conv_step{m}") for m in range(KC)]
        y_headed = sem("y_headed")
        y_split = sem("y_split")
        routed = sem("routed")
        residual_turned = sem("residual_turned")
        residual_ready = sem("residual_ready")
        top_found = sem("top_found")
        top_cast = sem("top_cast")
        margin_ready = sem("margin_ready")
        odds_ready = sem("odds_ready")
        shares_ready = sem("shares_ready")
        picks_ready = sem("picks_ready")
        gates_summed = sem("gates_summed")
        expanded = sem("expanded")
        silu_ready = sem("silu_ready")
        hidden_ready = sem("hidden_ready")
        hidden_headed = sem("hidden_headed")
        hidden_split = sem("hidden_split")
        contracted = sem("contracted")
        combined = sem("combined")
        stored = sem("stored")

        block = ctx.enter_context(nc.Block())

        @block.sync
        def _(sp):
            sp.dma_start(xT[:, :, 0:STEPS, :], x_t).then_inc(gru_loaded, 16)
            sp.dma_start(wih[:, :, :, :], w_ih).then_inc(gru_loaded, 16)
            sp.dma_start(state[:, :], h0).then_inc(gru_loaded, 16)
            sp.dma_start(whh[:, :, :, :], w_hh).then_inc(gru_loaded, 16)
            sp.dma_start(tab[:, :], tables).then_inc(consts_loaded, 16)
            sp.dma_start(taps_s[:, :, :], taps).then_inc(consts_loaded, 16)
            sp.dma_start(conv_bs[:, :], conv_b).then_inc(consts_loaded, 16)
            sp.dma_start(bo_s[:, :], bo).then_inc(consts_loaded, 16)
            sp.dma_start(arena[:, :], w_first).then_inc(first_loaded, 16)
            sp.dma_start(raw_qkv[:, :], w_qkv[0]).then_inc(qkv_loaded, 16)
            sp.dma_start(raw_o[:, :], w_o[0]).then_inc(o_loaded, 16)
            with sp.Fori(1, GROUPS - 1) as j:
                sp.wait_ge(v_w_ready, j)
                sp.dma_start(raw_qkv[:, :], w_qkv[bass.ds(j, 1)].rearrange("o p c -> p (o c)")).then_inc(qkv_loaded, 16)
                sp.wait_ge(o_w_ready, j + 1)
                sp.dma_start(raw_o[:, :], w_o[bass.ds(j, 1)].rearrange("o p c -> p (o c)")).then_inc(o_loaded, 16)
            with sp.Fori(0, QUARTERS) as n:
                sp.wait_ge(combined, n * (QTILES * EXPERTS) + QTILES * EXPERTS)
                sp.dma_start(out[bass.ds(n, 1)].rearrange("o q p c -> p (o q) c"), out_f).then_inc(stored, 16)
            sp.wait_ge(stored, 16 * (QUARTERS + 1))

        @block.tensor
        def _(pe):
            def three(ps, a_hi, a_lo, b_hi, b_lo, first, last):
                pe.matmul(ps, a_lo, b_hi, start=first, stop=False)
                pe.matmul(ps, a_hi, b_lo, start=False, stop=False)
                return pe.matmul(ps, a_hi, b_hi, start=False, stop=last)

            def gru_step(t, u):
                for c in range(CB):
                    pe.matmul(ps_o[BATCH * c:BATCH * (c + 1), u, 0:4 * CW], ones16[:, :], bias16[:, c, :],
                              start=True, stop=False, skip_group_check=True)
                pe.wait_ge(x_ready, t + 1)
                for k in range(KC):
                    for c in range(CB):
                        mm = pe.matmul(ps_o[BATCH * c:BATCH * (c + 1), u, 0:3 * CW], x_now[:, u, k, :], wih[:, k, c, :],
                                       start=False, stop=False, skip_group_check=True)
                mm.then_inc(x_projected, 1)
                pe.wait_ge(state_ready, t + 1)
                for k in range(KC):
                    for c in range(CB):
                        mm = pe.matmul(ps_o[BATCH * c:BATCH * (c + 1), u, CW:4 * CW], stateT[:, 1 - u, k, :],
                                       whh[:, k, c, :], start=False, stop=(k == KC - 1), skip_group_check=True)
                mm.then_inc(gates_ready, 1)

            pe.wait_ge(gru_loaded, 64)
            pe.wait_ge(bias_ready, 3)
            with pe.Fori(0, A_LOOPS) as i:
                for u in range(2):
                    gru_step(i * 2 + u, u)

            def project_qk(j, half):
                for pair in range(2):
                    if isinstance(j, int) and 4 * j + 2 * half + pair < 2:
                        pass
                    else:
                        pe.wait_ge(qk_products, j * 4 + (2 * half + pair - 1))
                    for part in range(2):
                        for k in range(KC):
                            cols = slice(part * P, part * P + P)
                            mm = three(ps_qk[:, 2 * pair + part, :],
                                       qkv_w(w_hi, pair, k)[:, cols], qkv_w(w_lo, pair, k)[:, cols],
                                       hs_hi[:, k, half * BH:(half + 1) * BH, :], hs_lo[:, k, half * BH:(half + 1) * BH, :],
                                       k == 0, k == KC - 1)
                    mm.then_inc(qk_projected, 1)

            def project_v(j):
                for n in range(TILES // 2):
                    if isinstance(j, int) and j == 0:
                        if n >= 2:
                            pe.wait_ge(v_ready, n - 1)
                    elif n < 2:
                        pe.wait_ge(o_split, j * 4 + (n - 1))
                    else:
                        pe.wait_ge(v_ready, j * 4 + (n - 1))
                    for h in range(2):
                        tile = 2 * n + h
                        seqs = slice(tile * TILE_B, (tile + 1) * TILE_B)
                        for k in range(KC):
                            mm = three(ps_o[:, n % 2, h * VW:(h + 1) * VW],
                                       hs_hi[:, k, seqs, :], hs_lo[:, k, seqs, :],
                                       qkv_w(w_hi, 2, k), qkv_w(w_lo, 2, k), k == 0, k == KC - 1)
                    mm.then_inc(v_projected, 1)

            def score(g, half):
                pe.wait_ge(k_spread, g * 2 + (half + 1))
                pe.wait_ge(qk_rotated, g * 4 + (2 * half + 2))
                for tile in range(TILES_H):
                    for part in range(2):
                        for b in range(TILE_B):
                            seq = half * BH + tile * TILE_B + b
                            mm = pe.matmul(ps_s[STEPS * b:STEPS * (b + 1), half, tile * P:(tile + 1) * P],
                                           q_s[:, part, seq, :], k_bd[:, part, seq, :, :],
                                           start=(part == 0), stop=(part == 1), skip_group_check=True)
                mm.then_inc(scored, 1)

            def attend(g, half):
                pe.wait_ge(prob_turned, g * 2 + (half + 1))
                if half == 0:
                    pe.wait_ge(v_ready, g * 4 + 4)
                for hp in range(HP):
                    if half == 1:
                        pe.wait_ge(o_split, g * 4 + (hp + 1))
                    for tile in range(TILES_H):
                        for e in range(2):
                            head = 2 * hp + e
                            mm = pe.matmul(ps_o[HEAD_DIM * e:HEAD_DIM * (e + 1), hp, tile * P:(tile + 1) * P],
                                           v_s[:, half * TILES_H + tile, head * HEAD_DIM:(head + 1) * HEAD_DIM],
                                           p_bd[:, half, tile * PER_GROUP + head, :], start=True, stop=True,
                                           skip_group_check=True)
                    mm.then_inc(attended, 1)

            def project_o(g):
                for m in range(KC):
                    for half in range(2):
                        for hp in range(HP):
                            at = WO_AT + hp * DIM + m * P
                            mm = three(ps_qk[:, 2 * m + half, :], w_hi[:, at:at + P], w_lo[:, at:at + P],
                                       o_hi[:, hp, half * TH:(half + 1) * TH], o_lo[:, hp, half * TH:(half + 1) * TH],
                                       hp == 0, hp == HP - 1)
                        mm.then_inc(o_projected, 1)

            pe.wait_ge(w_split, A_LOOPS)
            pe.wait_ge(hs_saved, STEPS + 2)
            project_qk(0, 0)
            project_qk(0, 1)
            project_v(0)
            with pe.Fori(0, GROUPS - 1) as g:
                score(g, 0)
                pe.wait_ge(qk_w_ready, g + 1)
                pe.wait_ge(x2_updated, g * 4 + 4)
                project_qk(g + 1, 0)
                score(g, 1)
                project_qk(g + 1, 1)
                attend(g, 0)
                attend(g, 1)
                pe.wait_ge(v_w_ready, g + 1)
                project_v(g + 1)
                pe.wait_ge(o_split, g * 4 + 4)
                pe.wait_ge(qk_products, g * 4 + 8)
                pe.wait_ge(o_w_ready, g + 1)
                project_o(g)
            last = GROUPS - 1
            score(last, 0)
            score(last, 1)
            attend(last, 0)
            attend(last, 1)
            pe.wait_ge(o_split, 4 * GROUPS)
            pe.wait_ge(x2_updated, 4 * GROUPS)
            pe.wait_ge(o_w_ready, GROUPS)
            project_o(last)

            def expand(e):
                for n, at in enumerate((W1_AT, W2_AT)):
                    for k in range(KC):
                        a = at + (e * KC + k) * FF
                        mm = three(ps_s[:, e % 2, n * QT:(n + 1) * QT], w_hi[:, a:a + FF], w_lo[:, a:a + FF],
                                   y_hi[:, k, :], y_lo[:, k, :], k == 0, k == KC - 1)
                mm.then_inc(expanded, 1)

            def contract(e):
                a = W3_AT + e * DIM
                for q in range(QTILES):
                    mm = three(ps_o[:, e % 2, q * DIM:(q + 1) * DIM],
                               hid_hi[:, e % 2, q * P:(q + 1) * P], hid_lo[:, e % 2, q * P:(q + 1) * P],
                               w_hi[:, a:a + DIM], w_lo[:, a:a + DIM], True, True)
                mm.then_inc(contracted, 1)

            pe.wait_ge(consts_loaded, 64)
            pe.wait_ge(x2_updated, 4 * GROUPS + 4)
            with pe.Fori(0, QUARTERS) as n:
                pe.wait_ge(quarter_copied, n + 1)
                for q in range(QTILES):
                    for m in range(KC):
                        mm = pe.matmul(ps_qk[:, 1, q * DIM + m * P:q * DIM + (m + 1) * P],
                                       x2_q[:, m, q * P:(q + 1) * P], ident, start=True, stop=True)
                mm.then_inc(residual_turned, 1)
                pe.wait_ge(y_split, n + 1)
                for q in range(QTILES):
                    for k in range(KC):
                        a = RW_AT + k * EXPERTS
                        mm = three(ps_qk[:, 0, q * EXPERTS:(q + 1) * EXPERTS],
                                   y_hi[:, k, q * P:(q + 1) * P], y_lo[:, k, q * P:(q + 1) * P],
                                   w_hi[:, a:a + EXPERTS], w_lo[:, a:a + EXPERTS], k == 0, k == KC - 1)
                mm.then_inc(routed, 1)
                for e in range(EXPERTS + 2):
                    if e < EXPERTS:
                        if e >= 2:
                            pe.wait_ge(hidden_ready, n * EXPERTS + (e - 1))
                        expand(e)
                    if e >= 2:
                        pe.wait_ge(hidden_split, n * EXPERTS + (e - 1))
                        if e >= 4:
                            pe.wait_ge(combined, n * (QTILES * EXPERTS) + QTILES * (e - 3))
                        contract(e - 2)

        @block.scalar
        def _(act):
            act.wait_ge(bias_zeroed, 1)
            for row in (0, 32):
                act.dma_start(bias_raw[row:row + 2, :, :], gate_bias).then_inc(bias_loaded, 16)
            nc.scalar.preload_act_table(ACT.Exp)
            act.wait_ge(gru_loaded, 64)
            act.wait_ge(consts_loaded, 64)

            with act.Fori(0, A_LOOPS) as i:
                for u in range(2):
                    t = i * 2 + u
                    act.wait_ge(gates_ready, t + 1)
                    nc.scalar.activation(rz[:, :], ps_o[:, u, CW:3 * CW], ACT.Tanh, scale=0.5).then_inc(rz_ready, 1)
                    act.wait_ge(cand_summed, t + 1)
                    nc.scalar.activation(cand[:, 2, :], cand[:, 1, :], ACT.Tanh).then_inc(cand_ready, 1)

            for m in range(KC):
                nc.scalar.activation(x2[:, m, :, :], xT[:, m, 0:STEPS, :].rearrange("p t b -> p b t"), ACT.Identity,
                                     bias=bo_s[:, m:m + 1]).then_inc(x2_updated, 2)

            def spread_k(j, half):
                act.wait_ge(qk_rotated, j * 4 + (2 * half + 2))
                for h in range(PER_GROUP):
                    rows = slice(HALF * h, HALF * (h + 1))
                    last = nc.scalar.copy(k_bd[rows, :, half * BH:(half + 1) * BH, h, :],
                                          k_s[rows, :, half * BH:(half + 1) * BH, :])
                last.then_inc(k_spread, 1)

            def exponent(g, half):
                act.wait_ge(shifted, g * 2 + (half + 1))
                nc.scalar.activation(prob[:, half, :, :], soft[:, half, :, :], ACT.Exp).then_inc(exp_ready, 1)

            def head_o(g, n):
                act.wait_ge(attended, g * 4 + (n + 1))
                half, hp = n // 2, n % 2
                nc.scalar.copy(o_hi[:, hp, half * TH:(half + 1) * TH], ps_o[:, hp, :]).then_inc(o_headed, 1)

            def take_v(j):
                for n in range(TILES // 2):
                    act.wait_ge(v_projected, j * 4 + (n + 1))
                    nc.scalar.copy(v_s[:, 2 * n:2 * n + 2, :], ps_o[:, n % 2, :]).then_inc(v_ready, 1)

            act.wait_ge(k_diag_zeroed, 1)
            spread_k(0, 0)
            spread_k(0, 1)
            take_v(0)
            with act.Fori(0, GROUPS - 1) as g:
                exponent(g, 0)
                exponent(g, 1)
                spread_k(g + 1, 0)
                head_o(g, 0)
                head_o(g, 1)
                spread_k(g + 1, 1)
                head_o(g, 2)
                head_o(g, 3)
                take_v(g + 1)
            exponent(GROUPS - 1, 0)
            exponent(GROUPS - 1, 1)
            for n in range(4):
                head_o(GROUPS - 1, n)

            nc.scalar.preload_act_table(ACT.Silu)
            act.wait_ge(x2_updated, 4 * GROUPS + 4)
            nc.scalar.copy(x2_q, x2[:, :, 0:QB, :].rearrange("p m b t -> p m (b t)")).then_inc(quarter_copied, 1)

            def quarter(n, more):
                for m in range(KC):
                    act.wait_ge(conv_step[m], n * TAPS + TAPS)
                nc.scalar.copy(y_hi[:, :, :], y_f.rearrange("p m b t -> p m (b t)")).then_inc(y_headed, 1)
                act.wait_ge(residual_turned, n + 1)
                act.wait_ge(stored, n * 16 + 16)
                nc.scalar.copy(out_f, ps_qk[:, 1, :]).then_inc(residual_ready, 1)
                if more:
                    nc.scalar.copy(x2_q, x2[:, :, bass.ds(n * QB + QB, QB), :].rearrange("p m b t -> p m (b t)"))\
                        .then_inc(quarter_copied, 1)
                act.wait_ge(margin_ready, n + 1)
                nc.scalar.activation(route[:, :, 1:2], route[:, :, 0:1], ACT.Tanh, scale=0.5 / SPLIT).then_inc(odds_ready, 1)
                for e in range(EXPERTS + 1):
                    if e < EXPERTS:
                        act.wait_ge(expanded, n * EXPERTS + (e + 1))
                        if e >= 2:
                            act.wait_ge(hidden_ready, n * EXPERTS + (e - 1))
                        nc.scalar.activation(gate_f[:, e % 2, :], ps_s[:, e % 2, 0:QT], ACT.Silu, scale=1.0 / SPLIT)\
                            .then_inc(silu_ready, 1)
                    if e >= 1:
                        act.wait_ge(hidden_ready, n * EXPERTS + e)
                        if e >= 3:
                            act.wait_ge(contracted, n * EXPERTS + (e - 2))
                        nc.scalar.copy(hid_hi[:, (e - 1) % 2, :], hid_f[:, (e - 1) % 2, :]).then_inc(hidden_headed, 1)

            with act.Fori(0, QUARTERS - 1) as n:
                quarter(n, True)
            quarter(QUARTERS - 1, False)

        @block.vector
        def _(dve):
            nc.vector.memset(bias_raw[:, :, :], 0.0).then_inc(bias_zeroed, 1)
            nc.vector.memset(ones16[:, :], 1.0).then_inc(bias_ready, 1)
            nc.vector.memset(k_bd[:, 0, :, :, :], 0.0).then_inc(stored, 16)
            nc.vector.memset(k_bd[:, 1, :, :, :], 0.0).then_inc(k_diag_zeroed, 1)
            dve.wait_ge(bias_loaded, 32)
            nc.vector.tensor_copy(bias16[:, :, :], bias_raw[:, :, :]).then_inc(bias_ready, 1)
            dve.wait_ge(bias_ready, 2)
            nc.vector.tensor_tensor(bias16[32:64, :, :], bias_raw[32:64, :, :], bias16[32:64, :, :], ALU.subtract)\
                .then_inc(bias_ready, 1)
            dve.wait_ge(gru_loaded, 64)
            nc.vector.transpose(stateT[:, 1, :, :].rearrange("p e b -> p (e b)"), state[:, :]).then_inc(state_ready, 1)

            with dve.Fori(0, A_LOOPS) as i:
                for u in range(2):
                    t = i * 2 + u
                    r, z = rz[:, 0:CW], rz[:, CW:2 * CW]
                    dve.wait_ge(rz_ready, t + 1)
                    nc.vector.scalar_tensor_tensor(cand[:, 0, :], r, 1.0, ps_o[:, u, 3 * CW:4 * CW], ALU.add, ALU.mult)\
                        .then_inc(reset_done, 1)
                    nc.vector.tensor_scalar(blend[:, 0, :], z, -0.5, 0.5, ALU.mult, ALU.add)
                    dve.wait_ge(reset_done, t + 1)
                    nc.vector.scalar_tensor_tensor(cand[:, 1, :], cand[:, 0, :], 0.5, ps_o[:, u, 0:CW], ALU.mult, ALU.add)\
                        .then_inc(cand_summed, 1)
                    nc.vector.tensor_scalar(blend[:, 1, :], z, 0.5, 0.5, ALU.mult, ALU.add).then_inc(z_ready, 1)
                    dve.wait_ge(z_ready, t + 1)
                    nc.vector.tensor_tensor(blend[:, 2, :], blend[:, 1, :], state[:, :], ALU.mult).then_inc(blend_ready, 1)
                    dve.wait_ge(cand_ready, t + 1)
                    nc.vector.tensor_tensor(blend[:, 3, :], cand[:, 2, :], blend[:, 0, :], ALU.mult).then_inc(blend_ready, 1)
                    dve.wait_ge(blend_ready, t * 2 + 2)
                    nc.vector.tensor_tensor(state[:, :], blend[:, 3, :], blend[:, 2, :], ALU.add).then_inc(state_new, 1)
                    dve.wait_ge(hs_saved, t + 1)
                    dve.wait_ge(state_new, t + 1)
                    nc.vector.transpose(stateT[:, u, :, :].rearrange("p e b -> p (e b)"), state[:, :]).then_inc(state_ready, 1)

            def rotate(j, half, pair):
                n = 2 * half + pair
                dve.wait_ge(qk_projected, j * 4 + (n + 1))
                if isinstance(j, int) and j == 0:
                    if n >= 2:
                        dve.wait_ge(qk_rotated, n - 1)
                else:
                    dve.wait_ge(qk_rotated, j * 4 + (n - 1))
                cos, sin, neg = rot[3 * pair:3 * pair + 3]
                src = ps_qk[:, 2 * pair:2 * pair + 2, :].rearrange("p a (b t) -> p a b t", b=BH)
                into = prods[:, pair, :, :].rearrange("p n (a b t) -> p n a b t", a=2, b=BH)
                nc.vector.tensor_tensor(into[:, 0].rearrange("p a b t -> p (a b) t"), src.rearrange("p a b t -> p (a b) t"),
                                        over(cos, 2 * BH), ALU.mult)
                nc.vector.tensor_tensor(into[:, 1, 0], src[:, 1], over(neg, BH), ALU.mult)
                nc.vector.tensor_tensor(into[:, 1, 1], src[:, 0], over(sin, BH), ALU.mult).then_inc(qk_products, 1)

            rows = TILES_H * PER_GROUP

            def wide(a, half):
                return stats[:, half, a, :].rearrange("p (r o) -> p r o", o=1).broadcast_to([P, rows, STEPS])

            def softmax_front(g, half):
                dve.wait_ge(scored, g * 2 + (half + 1))
                nc.vector.tensor_tensor(soft[:, half, :, :], ps_s[:, half, :].rearrange("p (r t) -> p r t", t=STEPS),
                                        over(mask, rows), ALU.add).then_inc(masked, 1)
                dve.wait_ge(masked, g * 2 + (half + 1))
                nc.vector.tensor_reduce(stats[:, half, 0, :], soft[:, half, :, :], AX.X, ALU.max).then_inc(max_ready, 1)
                dve.wait_ge(max_ready, g * 2 + (half + 1))
                nc.vector.tensor_tensor(soft[:, half, :, :], soft[:, half, :, :], wide(0, half), ALU.subtract)\
                    .then_inc(shifted, 1)

            dve.wait_ge(pool_set, 1)

            def softmax_back(g, half):
                dve.wait_ge(exp_ready, g * 2 + (half + 1))
                nc.vector.tensor_reduce(stats[:, half, 1, :], prob[:, half, :, :], AX.X, ALU.add).then_inc(sum_ready, 1)
                dve.wait_ge(sum_ready, g * 2 + (half + 1))
                nc.vector.reciprocal(stats[:, half, 2, :], stats[:, half, 1, :]).then_inc(rsum_ready, 1)
                dve.wait_ge(rsum_ready, g * 2 + (half + 1))
                nc.vector.tensor_tensor(soft[:, half, :, :], prob[:, half, :, :], wide(2, half), ALU.mult)\
                    .then_inc(prob_ready, 1)
                dve.wait_ge(prob_ready, g * 2 + (half + 1))
                for b in range(TILE_B):
                    part = slice(STEPS * b, STEPS * (b + 1))
                    last = nc.vector.transpose(p_bd[part, half, :, STEPS * b:STEPS * (b + 1)], soft[part, half, :, :])
                last.then_inc(prob_turned, 1)

            def tail_o(g, n):
                half, hp = n // 2, n % 2
                dve.wait_ge(o_headed, g * 4 + (n + 1))
                cols = slice(half * TH, (half + 1) * TH)
                nc.vector.tensor_tensor(o_lo[:, hp, cols], ps_o[:, hp, :], o_hi[:, hp, cols], ALU.subtract)\
                    .then_inc(o_split, 1)

            def add_o(g):
                dve.wait_ge(x2_updated, g * 4 + 4)
                for m in range(KC):
                    for half in range(2):
                        dve.wait_ge(o_projected, g * 4 + (2 * m + half + 1))
                        part = x2[:, m, half * BH:(half + 1) * BH, :].rearrange("p b t -> p (b t)")
                        nc.vector.scalar_tensor_tensor(part, ps_qk[:, 2 * m + half, :], 1.0 / (SPLIT * SPLIT), part,
                                                       ALU.mult, ALU.add).then_inc(x2_updated, 1)

            dve.wait_ge(consts_loaded, 64)
            for half in range(2):
                for pair in range(2):
                    rotate(0, half, pair)
            with dve.Fori(0, GROUPS - 1) as g:
                for half in range(2):
                    softmax_front(g, half)
                    rotate(g + 1, half, 0)
                    softmax_back(g, half)
                    rotate(g + 1, half, 1)
                for n in range(4):
                    tail_o(g, n)
                add_o(g)
            last_g = GROUPS - 1
            softmax_front(last_g, 0)
            softmax_front(last_g, 1)
            softmax_back(last_g, 0)
            softmax_back(last_g, 1)
            for n in range(4):
                tail_o(last_g, n)
            add_o(last_g)

            x2_qv = x2_q.rearrange("p m (b t) -> p m b t", b=QB)

            def convolve(n, lags):
                for lag in lags:
                    for m in range(KC):
                        w = taps_s[:, m, TAPS - 1 - lag:TAPS - lag]
                        if lag == 0:
                            nc.vector.tensor_scalar(y_f[:, m], x2_qv[:, m], w, conv_bs[:, m:m + 1], ALU.mult, ALU.add)\
                                .then_inc(conv_step[m], 1)
                            continue
                        dve.wait_ge(conv_step[m], n * TAPS + lag)
                        nc.vector.scalar_tensor_tensor(y_f[:, m, :, lag:], x2_qv[:, m, :, 0:STEPS - lag], w,
                                                       y_f[:, m, :, lag:], ALU.mult, ALU.add).then_inc(conv_step[m], 1)

            def choose(n):
                dve.wait_ge(routed, n + 1)
                nc.vector.tensor_copy(logits[:, :, :], ps_qk[:, 0, 0:QTILES * EXPERTS].rearrange("p (q e) -> p q e", q=QTILES))
                dve.drain()
                for q in range(QTILES):
                    nc.vector.max(top[:, q, :], logits[:, q, :])
                dve.drain()
                for q in range(QTILES):
                    nc.vector.max_index(top_at[:, q, :], top[:, q, :], logits[:, q, :]).then_inc(top_found, 1)
                nc.vector.tensor_tensor(route[:, :, 0:1], top[:, :, 0:1], top[:, :, 1:2], ALU.subtract)\
                    .then_inc(margin_ready, 1)
                dve.wait_ge(top_found, n * QTILES + QTILES)
                nc.vector.tensor_copy(top_f[:, :, :], top_at[:, :, :]).then_inc(top_cast, 1)
                dve.wait_ge(odds_ready, n + 1)
                nc.vector.tensor_scalar(route[:, :, 2:3], route[:, :, 1:2], 0.5 / SPLIT, 0.5 / SPLIT, ALU.mult, ALU.add)
                nc.vector.tensor_scalar(route[:, :, 3:4], route[:, :, 1:2], -0.5 / SPLIT, 0.5 / SPLIT, ALU.mult, ALU.add)\
                    .then_inc(shares_ready, 1)
                dve.wait_ge(top_cast, n + 1)
                dve.wait_ge(shares_ready, n + 1)
                for q in range(QTILES):
                    for s in range(2):
                        last = nc.vector.tensor_scalar(pick[:, q, s, :], iota, top_f[:, q, s:s + 1], route[:, q, 2 + s:3 + s],
                                                       ALU.is_equal, ALU.mult)
                last.then_inc(picks_ready, 1)
                dve.wait_ge(picks_ready, n + 1)
                nc.vector.tensor_tensor(pick[:, :, 2, :], pick[:, :, 0, :], pick[:, :, 1, :], ALU.add).then_inc(gates_summed, 1)
                dve.wait_ge(gates_summed, n + 1)

            def hidden(n, e):
                dve.wait_ge(silu_ready, n * EXPERTS + (e + 1))
                if e >= 2:
                    dve.wait_ge(hidden_split, n * EXPERTS + (e - 1))
                nc.vector.scalar_tensor_tensor(hid_f[:, e % 2, :], ps_s[:, e % 2, QT:2 * QT], 1.0 / SPLIT,
                                               gate_f[:, e % 2, :], ALU.mult, ALU.mult).then_inc(hidden_ready, 1)

            def combine(n, e):
                dve.wait_ge(contracted, n * EXPERTS + (e + 1))
                if e == 0:
                    dve.wait_ge(residual_ready, n + 1)
                else:
                    dve.wait_ge(combined, n * (QTILES * EXPERTS) + QTILES * e)
                for q in range(QTILES):
                    nc.vector.scalar_tensor_tensor(out_f[:, q, :], ps_o[:, e % 2, q * DIM:(q + 1) * DIM],
                                                   pick[:, q, 2, e:e + 1], out_f[:, q, :], ALU.mult, ALU.add)\
                        .then_inc(combined, 1)

            def quarter(n, more):
                choose(n)
                for e in range(EXPERTS + 2):
                    if e < EXPERTS:
                        hidden(n, e)
                    if more and e < EXPERTS:
                        if e == 0:
                            dve.wait_ge(quarter_copied, n + 2)
                            dve.wait_ge(y_split, n + 1)
                        convolve(n + 1, range(TAPS // EXPERTS * e, TAPS // EXPERTS * (e + 1)))
                    if e >= 2:
                        combine(n, e - 2)

            dve.wait_ge(quarter_copied, 1)
            convolve(0, range(TAPS))
            with dve.Fori(0, QUARTERS - 1) as n:
                quarter(n, True)
            quarter(QUARTERS - 1, False)

        @block.gpsimd
        def _(pool):
            nc.gpsimd.memset(split_by[:, :], SPLIT).then_inc(hs_saved, 2)
            nc.gpsimd.memset(xT[:, :, STEPS:STEPS + 2, :], 0.0).then_inc(o_w_ready, 1)
            nc.gpsimd.memset(p_bd[:, :, :, :], 0.0).then_inc(pool_set, 1)
            pool.wait_ge(pool_set, 1)
            pool.wait_ge(gru_loaded, 64)
            for u in range(2):
                nc.gpsimd.tensor_copy(x_now[:, u, :, :], xT[:, :, u, :]).then_inc(x_ready, 1)
            pool.wait_ge(first_loaded, 16)
            with pool.Fori(0, A_LOOPS) as i:
                cols = bass.ds(i * SPLIT_STEP, SPLIT_STEP)
                for u in range(2):
                    t = i * 2 + u
                    now = bass.ds(t, 1)
                    pool.wait_ge(x_projected, t + 1)
                    nc.gpsimd.tensor_copy(x_now[:, u, :, :], xT[:, :, bass.ds(t + 2, 1), :].rearrange("p k o b -> p k (o b)"))\
                        .then_inc(x_ready, 1)
                    pool.wait_ge(state_ready, t + 2)
                    hi = hs_hi[:, :, :, now].rearrange("p k b o -> p k (b o)")
                    lo = hs_lo[:, :, :, now].rearrange("p k b o -> p k (b o)")
                    nc.gpsimd.tensor_copy(hi, stateT[:, u, :, :]).then_inc(hs_hi_saved, 1)
                    if u == 0:
                        nc.gpsimd.tensor_tensor(arena[:, cols], arena[:, cols],
                                                split_by[:, 0:1].broadcast_to([P, SPLIT_STEP]), ALU.mult).then_inc(w_scaled, 1)
                    pool.wait_ge(hs_hi_saved, t + 1)
                    nc.gpsimd.tensor_tensor(lo, stateT[:, u, :, :], hi, ALU.subtract).then_inc(hs_saved, 1)
                    if u == 0:
                        pool.wait_ge(w_scaled, i + 1)
                        nc.gpsimd.tensor_copy(w_hi[:, cols], arena[:, cols]).then_inc(w_headed, 1)
                    else:
                        pool.wait_ge(w_headed, i + 1)
                        nc.gpsimd.tensor_tensor(w_lo[:, cols], arena[:, cols], w_hi[:, cols], ALU.subtract)\
                            .then_inc(w_split, 1)

            def add_products(j, half, pair):
                n = 2 * half + pair
                pool.wait_ge(qk_products, j * 4 + (n + 1))
                into = (q_s, k_s)[pair][:, :, half * BH:(half + 1) * BH, :].rearrange("p a b t -> p a (b t)")
                both = prods[:, pair, :, :].rearrange("p n (a c) -> p n a c", a=2)
                nc.gpsimd.tensor_tensor(into, both[:, 0], both[:, 1], ALU.add).then_inc(qk_rotated, 1)

            qkv_view = raw_qkv[:, :].rearrange("p (k c) -> p k c", k=KC)

            def split_part(w, lo, hi):
                return w[:, QKV_AT:QKV_AT + QKV_COLS].rearrange("p (k c) -> p k c", k=KC)[:, :, lo:hi]

            def split_cols(raw, head, tail, order, ready):
                by = split_by[:, 0:1]
                by = by.broadcast_to([P, raw.shape[1]]) if len(raw.shape) == 2 else \
                    by.rearrange("p (o c) -> p o c", o=1).broadcast_to([P, raw.shape[1], raw.shape[2]])
                nc.gpsimd.tensor_tensor(head, raw, by, ALU.mult).then_inc(w_headed, 1)
                pool.wait_ge(w_headed, order)
                nc.gpsimd.tensor_tensor(raw, raw, by, ALU.mult).then_inc(w_scaled, 1)
                pool.wait_ge(w_scaled, order)
                nc.gpsimd.tensor_tensor(tail, raw, head, ALU.subtract).then_inc(ready, 1)

            def split_qkv(j, order):
                pool.wait_ge(qkv_loaded, j * 16)
                pool.wait_ge(qk_projected, j * 4)
                split_cols(qkv_view[:, :, 0:2 * DIM], split_part(w_hi, 0, 2 * DIM), split_part(w_lo, 0, 2 * DIM), order,
                           qk_w_ready)
                pool.wait_ge(v_projected, j * 4)
                split_cols(qkv_view[:, :, 2 * DIM:], split_part(w_hi, 2 * DIM, 3 * DIM), split_part(w_lo, 2 * DIM, 3 * DIM),
                           order + 1, v_w_ready)

            def split_o(j, order):
                pool.wait_ge(o_loaded, j * 16)
                pool.wait_ge(o_projected, j * 4)
                split_cols(raw_o[:, :], w_hi[:, WO_AT:WO_AT + WO_COLS], w_lo[:, WO_AT:WO_AT + WO_COLS], order, o_w_ready)

            for half in range(2):
                for pair in range(2):
                    add_products(0, half, pair)
            split_qkv(1, A_LOOPS + 1)
            with pool.Fori(0, GROUPS - 2) as g:
                for half in range(2):
                    for pair in range(2):
                        add_products(g + 1, half, pair)
                split_qkv(g + 2, g * 3 + (A_LOOPS + 3))
                split_o(g + 1, g * 3 + (A_LOOPS + 5))
            g = GROUPS - 2
            for half in range(2):
                for pair in range(2):
                    add_products(g + 1, half, pair)
            split_o(g + 1, g * 3 + (A_LOOPS + 3))

            def quarter(n):
                pool.wait_ge(y_headed, n + 1)
                nc.gpsimd.tensor_tensor(y_lo[:, :, :], y_f.rearrange("p m b t -> p m (b t)"), y_hi[:, :, :], ALU.subtract)\
                    .then_inc(y_split, 1)
                for e in range(EXPERTS):
                    pool.wait_ge(hidden_headed, n * EXPERTS + (e + 1))
                    nc.gpsimd.tensor_tensor(hid_lo[:, e % 2, :], hid_f[:, e % 2, :], hid_hi[:, e % 2, :], ALU.subtract)\
                        .then_inc(hidden_split, 1)

            with pool.Fori(0, QUARTERS) as n:
                quarter(n)


def _tables(np):
    inv = (1.0 / 10000.0 ** (np.arange(0, HEAD_DIM, 2, dtype=np.float32) / np.float32(HEAD_DIM))).astype(np.float32)
    angle = (np.arange(STEPS, dtype=np.float32)[None, :] * inv[:, None]).astype(np.float32)
    cos, sin = np.cos(angle).astype(np.float32), np.sin(angle).astype(np.float32)
    t = np.zeros((P, TAB_COLS), np.float32)
    for pair, scale in enumerate((HEAD_DIM ** -0.5 / SPLIT, 1.0 / SPLIT)):
        for n, table in enumerate((cos, sin, -sin)):
            at = (3 * pair + n) * STEPS
            t[:, at:at + STEPS] = np.tile(table * np.float32(scale), (P // HALF, 1))
    q, k = np.arange(P)[:, None] % STEPS, np.arange(STEPS)[None, :]
    t[:, TAB_MASK:TAB_MASK + STEPS] = np.where(q >= k, 0.0, -1e30)
    t[:, TAB_IDENT:TAB_IDENT + P] = np.eye(P)
    t[:, TAB_IOTA:] = np.arange(EXPERTS)
    return t


def kernel(**inputs):
    import numpy as np
    import concourse.bacc as _bacc
    from concourse.bass_utils import run_bass_kernel_spmd as _run

    a = {n: np.asarray(v) for n, v in inputs.items()}
    con = np.ascontiguousarray

    x_t = con(a["x"].transpose(2, 1, 0).reshape(KC, P, STEPS, BATCH).transpose(1, 0, 2, 3))
    h0 = con(a["cond_2048"].reshape(BATCH, CB, CW).transpose(1, 0, 2).reshape(P, CW))
    w_ih = con(a["L0_cond_W_ih"].reshape(KC, P, 3, CB, CW).transpose(1, 0, 3, 2, 4)[:, :, :, [2, 0, 1]]
               .reshape(P, KC, CB, 3 * CW))

    def state_rows(w):
        return w.reshape(CB, KC, 32, -1).transpose(0, 2, 1, 3).reshape(P, KC, -1)

    w_hh = con(state_rows(a["L0_cond_W_hh"]).reshape(P, KC, 3, CB, CW).transpose(0, 1, 3, 2, 4)
               .reshape(P, KC, CB, 3 * CW))
    bi, bh = (a[n].reshape(3, CB, CW) for n in ("L0_cond_b_ih", "L0_cond_b_hh"))
    gate_bias = np.zeros((2, CB, 4 * CW), np.float32)
    for n, g in enumerate((2, 0, 1)):
        gate_bias[0, :, n * CW:(n + 1) * CW] = bi[g]
    for n, g in enumerate((0, 1, 2)):
        gate_bias[1, :, (n + 1) * CW:(n + 2) * CW] = bh[g]

    def rotary_rows(w):
        return w.reshape(GROUPS, PER_GROUP, 2, HALF, DIM).transpose(0, 2, 1, 3, 4).reshape(GROUPS, DIM, DIM)

    qkv = np.stack([rotary_rows(a["L0_attn_Wq"]), rotary_rows(a["L0_attn_Wk"]),
                    a["L0_attn_Wv"].reshape(GROUPS, VW, DIM)], 1)
    qkv = qkv.transpose(0, 3, 1, 2)
    qkv = con(np.stack([state_rows(w) for w in qkv]).reshape(GROUPS, P, QKV_COLS))
    w_o = con(a["L0_attn_Wo"].T.reshape(GROUPS, HP, P, DIM).transpose(0, 2, 1, 3).reshape(GROUPS, P, WO_COLS))

    def up(w):
        return w.reshape(EXPERTS, KC, P, FF).transpose(2, 0, 1, 3).reshape(P, W1_COLS)

    w_first = con(np.concatenate([
        up(a["L0_ffn_w1"]), up(a["L0_ffn_w2"]), a["L0_ffn_w3"].transpose(1, 0, 2).reshape(P, W3_COLS),
        qkv[0], w_o[0], a["L0_ffn_router_w"].T.reshape(KC, P, EXPERTS).transpose(1, 0, 2).reshape(P, RW_COLS)], 1))
    arrays = {
        "x_t": x_t, "h0": h0, "w_ih": w_ih, "w_hh": w_hh, "gate_bias": gate_bias, "w_first": w_first,
        "w_qkv": con(qkv[1:]), "w_o": con(w_o[1:]),
        "bo": con(a["L0_attn_bo"].reshape(KC, P).T), "tables": _tables(np),
        "taps": con(a["cond_2048"].T.reshape(KC, P, TAPS).transpose(1, 0, 2)),
        "conv_b": con(a["L0_cond2_b"].reshape(KC, P).T),
    }
    nc = _bacc.Bacc("TRN2", target_bir_lowering=False, num_devices=1)
    args = [nc.dram_tensor(f"{n}_dram", v.shape, mybir.dt.from_np(v.dtype), kind="ExternalInput").ap()
            for n, v in arrays.items()]
    out = nc.dram_tensor("out_dram", (QUARTERS, QTILES, P, DIM), F32, kind="ExternalOutput").ap()
    block_kernel(nc, *args, out)
    r = _run(nc, [{f"{n}_dram": v for n, v in arrays.items()}], core_ids=[0])
    return r.results[0]["out_dram"].reshape(BATCH, STEPS, DIM)
```

```python
from contextlib import ExitStack

import concourse.bass as bass
from concourse import mybir

F32 = mybir.dt.float32
F16 = mybir.dt.float16
U32 = mybir.dt.uint32
ALU = mybir.AluOpType
ACT = mybir.ActivationFunctionType
AX = mybir.AxisListType

P = 128
BATCH, STEPS, DIM = 32, 32, 256
TOKENS = BATCH * STEPS
KC = DIM // P
HEADS, HEAD_DIM = 32, 64
HALF = HEAD_DIM // 2
PER_GROUP = P // HALF
GROUPS = HEADS // PER_GROUP
CB = 4
CW = DIM // CB
TILE_B = P // STEPS
TILES = TOKENS // P
BH = BATCH // 2
TH = TOKENS // 2
TILES_H = TILES // 2
HP = PER_GROUP // 2
VW = PER_GROUP * HEAD_DIM
EXPERTS, FF = 8, 128
TAPS = STEPS
QUARTERS = 4
QB = BATCH // QUARTERS
QT = TOKENS // QUARTERS
QTILES = QT // P
SPLIT = 256.0

QKV_COLS = KC * 3 * DIM
WO_COLS = HP * DIM
W1_COLS = EXPERTS * KC * FF
W3_COLS = EXPERTS * DIM
RW_COLS = KC * EXPERTS
W1_AT, W2_AT, W3_AT = 0, W1_COLS, 2 * W1_COLS
QKV_AT = W3_AT + W3_COLS
WO_AT = QKV_AT + QKV_COLS
RW_AT = WO_AT + WO_COLS
SPLIT_COLS = RW_AT + RW_COLS
A_LOOPS = STEPS // 2
SPLIT_STEP = SPLIT_COLS // A_LOOPS
assert SPLIT_STEP * A_LOOPS == SPLIT_COLS

ROT = 6
TAB_MASK = ROT * STEPS
TAB_IDENT = TAB_MASK + STEPS
TAB_IOTA = TAB_IDENT + P
TAB_COLS = TAB_IOTA + EXPERTS


def block_kernel(nc: bass.Bass, x_t, h0, w_ih, w_hh, gate_bias, w_first, w_qkv, w_o, bo, tables, taps, conv_b, out):
    ctx = ExitStack()
    with ctx:
        def sb(name, shape, dt=F32):
            return ctx.enter_context(nc.sbuf_tensor(name, shape, dt))

        def pb(name, shape):
            return ctx.enter_context(nc.psum_tensor(name, shape, F32))

        def sem(name):
            return ctx.enter_context(nc.semaphore(name))

        ps_s = pb("ps_s", [P, 2, 512])
        ps_qk = pb("ps_qk", [P, 4, 512])
        ps_o = pb("ps_o", [P, 2, 512])

        xT = sb("xT", [P, KC, STEPS + 2, BATCH])
        x2 = sb("x2", [P, KC, BATCH, STEPS])
        hs_hi = sb("hs_hi", [P, KC, BATCH, STEPS], F16)
        hs_lo = sb("hs_lo", [P, KC, BATCH, STEPS], F16)
        wih = sb("wih", [P, KC, CB, 3 * CW])
        whh = sb("whh", [P, KC, CB, 3 * CW])
        bias_raw = sb("bias_raw", [P, CB, 4 * CW])
        bias16 = sb("bias16", [P, CB, 4 * CW], F16)
        ones16 = sb("ones16", [P, BATCH], F16)
        x_now = sb("x_now", [P, 2, KC, BATCH])
        state = sb("state", [P, CW])
        stateT = sb("stateT", [P, 2, KC, BATCH])
        rz = sb("rz", [P, 2 * CW])
        cand = sb("cand", [P, 3, CW])
        blend = sb("blend", [P, 4, CW])
        arena = sb("arena", [P, SPLIT_COLS])
        w_hi = sb("w_hi", [P, SPLIT_COLS], F16)
        w_lo = sb("w_lo", [P, SPLIT_COLS], F16)
        split_by = sb("split_by", [P, 1])
        raw_qkv = sb("raw_qkv", [P, QKV_COLS])
        raw_o = sb("raw_o", [P, WO_COLS])
        tab = sb("tab", [P, TAB_COLS])
        bo_s = sb("bo_s", [P, KC])
        taps_s = sb("taps_s", [P, KC, TAPS])
        conv_bs = sb("conv_bs", [P, KC])
        k_bd = sb("k_bd", [P, 2, BATCH, PER_GROUP, STEPS])
        v_s = sb("v_s", [P, 2, TILES, VW])
        soft = sb("soft", [P, 2, TILES_H * PER_GROUP, STEPS])
        prob = sb("prob", [P, 2, TILES_H * PER_GROUP, STEPS])
        stats = sb("stats", [P, 2, 3, TILES_H * PER_GROUP])
        p_bd = sb("p_bd", [P, 2, TILES_H * PER_GROUP, P])
        o_hi = sb("o_hi", [P, HP, TOKENS], F16)
        o_lo = sb("o_lo", [P, HP, TOKENS], F16)

        qk_cols = 2 * TOKENS
        q_s = arena[:, 0:qk_cols].rearrange("p (a b t) -> p a b t", a=2, b=BATCH)
        k_s = arena[:, qk_cols:2 * qk_cols].rearrange("p (a b t) -> p a b t", a=2, b=BATCH)
        prods = arena[:, 2 * qk_cols:4 * qk_cols].rearrange("p (u n c) -> p u n c", u=2, n=2)
        c_f = k_bd[:, :, :, :, :].rearrange("p a b h t -> p (a b h t)")
        x2_q = c_f[:, 0:KC * QT].rearrange("p (m c) -> p m c", m=KC)
        y_f = c_f[:, 512:512 + KC * QT].rearrange("p (m b t) -> p m b t", m=KC, b=QB)
        gate_f = c_f[:, 1024:1536].rearrange("p (u c) -> p u c", u=2)
        hid_f = c_f[:, 1536:2048].rearrange("p (u c) -> p u c", u=2)
        out_f = c_f[:, 2048:2560].rearrange("p (q c) -> p q c", q=QTILES)
        y_hi = sb("y_hi", [P, KC, QT], F16)
        y_lo = sb("y_lo", [P, KC, QT], F16)
        gated_f = c_f[:, 2560:3584].rearrange("p (u q c) -> p u q c", u=2, q=QTILES)
        hid_hi = sb("hid_hi", [P, 2, QT], F16)
        hid_lo = sb("hid_lo", [P, 2, QT], F16)
        logits = sb("logits", [P, QTILES, EXPERTS])
        top = sb("top", [P, QTILES, 8])
        top_at = sb("top_at", [P, QTILES, 8], U32)
        top_f = sb("top_f", [P, QTILES, 8])
        route = sb("route", [P, QTILES, 4])
        pick = sb("pick", [P, QTILES, 3, EXPERTS])

        rot = [tab[:, n * STEPS:(n + 1) * STEPS] for n in range(ROT)]
        mask = tab[:, TAB_MASK:TAB_MASK + STEPS]
        ident = tab[:, TAB_IDENT:TAB_IDENT + P]
        iota = tab[:, TAB_IOTA:TAB_IOTA + EXPERTS]

        def qkv_w(w, kind, k):
            a = QKV_AT + (k * 3 + kind) * DIM
            return w[:, a:a + DIM]

        def over(table, n):
            return table.rearrange("p (o t) -> p o t", o=1).broadcast_to([P, n, STEPS])

        gru_loaded = sem("gru_loaded")
        bias_loaded = sem("bias_loaded")
        first_loaded = sem("first_loaded")
        consts_loaded = sem("consts_loaded")
        qkv_loaded = sem("qkv_loaded")
        o_loaded = sem("o_loaded")
        bias_zeroed = sem("bias_zeroed")
        bias_ready = sem("bias_ready")
        k_diag_zeroed = sem("k_diag_zeroed")
        pool_set = sem("pool_set")
        x_ready = sem("x_ready")
        x_projected = sem("x_projected")
        gates_ready = sem("gates_ready")
        rz_ready = sem("rz_ready")
        reset_done = sem("reset_done")
        cand_summed = sem("cand_summed")
        cand_ready = sem("cand_ready")
        z_ready = sem("z_ready")
        blend_ready = sem("blend_ready")
        state_new = sem("state_new")
        state_ready = sem("state_ready")
        hs_hi_saved = sem("hs_hi_saved")
        hs_saved = sem("hs_saved")
        w_scaled = sem("w_scaled")
        w_headed = sem("w_headed")
        w_split = sem("w_split")
        x2_updated = sem("x2_updated")
        qk_projected = sem("qk_projected")
        qk_products = sem("qk_products")
        qk_rotated = sem("qk_rotated")
        k_spread = sem("k_spread")
        qk_w_ready = sem("qk_w_ready")
        v_w_ready = sem("v_w_ready")
        o_w_ready = sem("o_w_ready")
        v_projected = sem("v_projected")
        v_ready = sem("v_ready")
        scored = sem("scored")
        masked = sem("masked")
        max_ready = sem("max_ready")
        shifted = sem("shifted")
        exp_ready = sem("exp_ready")
        sum_ready = sem("sum_ready")
        rsum_ready = sem("rsum_ready")
        prob_ready = sem("prob_ready")
        prob_turned = sem("prob_turned")
        attended = sem("attended")
        o_headed = sem("o_headed")
        o_split = sem("o_split")
        o_projected = sem("o_projected")
        quarter_copied = sem("quarter_copied")
        conv_step = [sem(f"conv_step{m}") for m in range(KC)]
        y_headed = sem("y_headed")
        y_split = sem("y_split")
        routed = sem("routed")
        residual_turned = sem("residual_turned")
        residual_ready = sem("residual_ready")
        top_found = sem("top_found")
        top_cast = sem("top_cast")
        margin_ready = sem("margin_ready")
        odds_ready = sem("odds_ready")
        shares_ready = sem("shares_ready")
        picks_ready = sem("picks_ready")
        gates_summed = sem("gates_summed")
        expanded = sem("expanded")
        silu_ready = sem("silu_ready")
        hidden_ready = sem("hidden_ready")
        hidden_headed = sem("hidden_headed")
        hidden_split = sem("hidden_split")
        contracted = sem("contracted")
        gated = sem("gated")
        combined = sem("combined")
        stored = sem("stored")

        block = ctx.enter_context(nc.Block())

        @block.sync
        def _(sp):
            sp.dma_start(xT[:, :, 0:STEPS, :], x_t).then_inc(gru_loaded, 16)
            sp.dma_start(wih[:, :, :, :], w_ih).then_inc(gru_loaded, 16)
            sp.dma_start(state[:, :], h0).then_inc(gru_loaded, 16)
            sp.dma_start(whh[:, :, :, :], w_hh).then_inc(gru_loaded, 16)
            sp.dma_start(tab[:, :], tables).then_inc(consts_loaded, 16)
            sp.dma_start(taps_s[:, :, :], taps).then_inc(consts_loaded, 16)
            sp.dma_start(conv_bs[:, :], conv_b).then_inc(consts_loaded, 16)
            sp.dma_start(bo_s[:, :], bo).then_inc(consts_loaded, 16)
            sp.dma_start(arena[:, :], w_first).then_inc(first_loaded, 16)
            sp.dma_start(raw_qkv[:, :], w_qkv[0]).then_inc(qkv_loaded, 16)
            sp.dma_start(raw_o[:, :], w_o[0]).then_inc(o_loaded, 16)
            with sp.Fori(1, GROUPS - 1) as j:
                sp.wait_ge(v_w_ready, j)
                sp.wait_ge(qk_w_ready, j)
                sp.dma_start(raw_qkv[:, :], w_qkv[bass.ds(j, 1)].rearrange("o p c -> p (o c)")).then_inc(qkv_loaded, 16)
                sp.wait_ge(o_w_ready, j + 1)
                sp.dma_start(raw_o[:, :], w_o[bass.ds(j, 1)].rearrange("o p c -> p (o c)")).then_inc(o_loaded, 16)
            with sp.Fori(0, QUARTERS) as n:
                sp.wait_ge(combined, n * EXPERTS + EXPERTS)
                sp.dma_start(out[bass.ds(n, 1)].rearrange("o q p c -> p (o q) c"), out_f).then_inc(stored, 16)
            sp.wait_ge(stored, 16 * (QUARTERS + 1))

        @block.tensor
        def _(pe):
            def three(ps, a_hi, a_lo, b_hi, b_lo, first, last):
                pe.matmul(ps, a_lo, b_hi, start=first, stop=False)
                pe.matmul(ps, a_hi, b_lo, start=False, stop=False)
                return pe.matmul(ps, a_hi, b_hi, start=False, stop=last)

            def gru_step(t, u):
                for c in range(CB):
                    pe.matmul(ps_o[BATCH * c:BATCH * (c + 1), u, 0:4 * CW], ones16[:, :], bias16[:, c, :],
                              start=True, stop=False, skip_group_check=True)
                pe.wait_ge(x_ready, t + 1)
                for k in range(KC):
                    for c in range(CB):
                        mm = pe.matmul(ps_o[BATCH * c:BATCH * (c + 1), u, 0:3 * CW], x_now[:, u, k, :], wih[:, k, c, :],
                                       start=False, stop=False, skip_group_check=True)
                mm.then_inc(x_projected, 1)
                pe.wait_ge(state_ready, t + 1)
                for k in range(KC):
                    for c in range(CB):
                        mm = pe.matmul(ps_o[BATCH * c:BATCH * (c + 1), u, CW:4 * CW], stateT[:, 1 - u, k, :],
                                       whh[:, k, c, :], start=False, stop=(k == KC - 1), skip_group_check=True)
                mm.then_inc(gates_ready, 1)

            pe.wait_ge(gru_loaded, 64)
            pe.wait_ge(bias_ready, 3)
            with pe.Fori(0, A_LOOPS) as i:
                for u in range(2):
                    gru_step(i * 2 + u, u)

            def project_qk(j, half):
                for pair in range(2):
                    if isinstance(j, int) and 4 * j + 2 * half + pair < 2:
                        pass
                    else:
                        pe.wait_ge(qk_products, j * 4 + (2 * half + pair - 1))
                    for part in range(2):
                        for k in range(KC):
                            cols = slice(part * P, part * P + P)
                            mm = three(ps_qk[:, 2 * pair + part, :],
                                       qkv_w(w_hi, pair, k)[:, cols], qkv_w(w_lo, pair, k)[:, cols],
                                       hs_hi[:, k, half * BH:(half + 1) * BH, :], hs_lo[:, k, half * BH:(half + 1) * BH, :],
                                       k == 0, k == KC - 1)
                    mm.then_inc(qk_projected, 1)

            def project_v(j):
                for n in range(TILES // 2):
                    if n >= 2:
                        pe.wait_ge(v_ready, j * 4 + (n - 1))
                    elif not (isinstance(j, int) and j < 2):
                        pe.wait_ge(o_split, (j - 1) * 4 + (n - 1))
                    for h in range(2):
                        tile = 2 * n + h
                        seqs = slice(tile * TILE_B, (tile + 1) * TILE_B)
                        for k in range(KC):
                            mm = three(ps_o[:, n % 2, h * VW:(h + 1) * VW],
                                       hs_hi[:, k, seqs, :], hs_lo[:, k, seqs, :],
                                       qkv_w(w_hi, 2, k), qkv_w(w_lo, 2, k), k == 0, k == KC - 1)
                    mm.then_inc(v_projected, 1)

            def score(g, half):
                pe.wait_ge(k_spread, g * 2 + (half + 1))
                pe.wait_ge(qk_rotated, g * 4 + (2 * half + 2))
                for tile in range(TILES_H):
                    for part in range(2):
                        for b in range(TILE_B):
                            seq = half * BH + tile * TILE_B + b
                            mm = pe.matmul(ps_s[STEPS * b:STEPS * (b + 1), half, tile * P:(tile + 1) * P],
                                           q_s[:, part, seq, :], k_bd[:, part, seq, :, :],
                                           start=(part == 0), stop=(part == 1), skip_group_check=True)
                mm.then_inc(scored, 1)

            def attend(g, par, half, banks_free):
                pe.wait_ge(prob_turned, g * 2 + (half + 1))
                if half == 0:
                    pe.wait_ge(v_ready, banks_free)
                for hp in range(HP):
                    if half == 1:
                        pe.wait_ge(o_split, g * 4 + (hp + 1))
                    for tile in range(TILES_H):
                        for e in range(2):
                            head = 2 * hp + e
                            mm = pe.matmul(ps_o[HEAD_DIM * e:HEAD_DIM * (e + 1), hp, tile * P:(tile + 1) * P],
                                           v_s[:, par, half * TILES_H + tile, head * HEAD_DIM:(head + 1) * HEAD_DIM],
                                           p_bd[:, half, tile * PER_GROUP + head, :], start=True, stop=True,
                                           skip_group_check=True)
                    mm.then_inc(attended, 1)

            def project_o(g):
                for m in range(KC):
                    for half in range(2):
                        for hp in range(HP):
                            at = WO_AT + hp * DIM + m * P
                            mm = three(ps_qk[:, 2 * m + half, :], w_hi[:, at:at + P], w_lo[:, at:at + P],
                                       o_hi[:, hp, half * TH:(half + 1) * TH], o_lo[:, hp, half * TH:(half + 1) * TH],
                                       hp == 0, hp == HP - 1)
                        mm.then_inc(o_projected, 1)

            def group(g, par, first=False, last=False):
                score(g, 0)
                score(g, 1)
                if not first:
                    pe.wait_ge(o_split, g * 4)
                    pe.wait_ge(o_w_ready, g)
                    pe.wait_ge(qk_products, g * 4 + 4)
                    project_o(g - 1)
                if not last:
                    pe.wait_ge(qk_w_ready, g + 1)
                    pe.wait_ge(x2_updated, g * 4 + 4)
                    project_qk(g + 1, 0)
                    pe.wait_ge(v_w_ready, g + 1)
                    project_v(g + 1)
                    project_qk(g + 1, 1)
                attend(g, par, 0, g * 4 + (4 if last else 8))
                attend(g, par, 1, None)

            pe.wait_ge(w_split, A_LOOPS)
            pe.wait_ge(hs_saved, STEPS + 2)
            project_qk(0, 0)
            project_v(0)
            project_qk(0, 1)
            group(0, 0, first=True)
            with pe.Fori(0, (GROUPS - 2) // 2) as i:
                for par in range(2):
                    group(i * 2 + (par + 1), 1 - par)
            group(GROUPS - 1, (GROUPS - 1) % 2, last=True)
            pe.wait_ge(o_split, 4 * GROUPS)
            pe.wait_ge(x2_updated, 4 * GROUPS)
            pe.wait_ge(o_w_ready, GROUPS)
            project_o(GROUPS - 1)

            def expand(e):
                for n, at in enumerate((W1_AT, W2_AT)):
                    for k in range(KC):
                        a = at + (e * KC + k) * FF
                        mm = three(ps_s[:, e % 2, n * QT:(n + 1) * QT], w_hi[:, a:a + FF], w_lo[:, a:a + FF],
                                   y_hi[:, k, :], y_lo[:, k, :], k == 0, k == KC - 1)
                mm.then_inc(expanded, 1)

            def contract(e):
                a = W3_AT + e * DIM
                for q in range(QTILES):
                    mm = three(ps_o[:, e % 2, q * DIM:(q + 1) * DIM],
                               hid_hi[:, e % 2, q * P:(q + 1) * P], hid_lo[:, e % 2, q * P:(q + 1) * P],
                               w_hi[:, a:a + DIM], w_lo[:, a:a + DIM], True, True)
                mm.then_inc(contracted, 1)

            pe.wait_ge(consts_loaded, 64)
            pe.wait_ge(x2_updated, 4 * GROUPS + 4)
            with pe.Fori(0, QUARTERS) as n:
                pe.wait_ge(quarter_copied, n + 1)
                for q in range(QTILES):
                    for m in range(KC):
                        mm = pe.matmul(ps_qk[:, 1, q * DIM + m * P:q * DIM + (m + 1) * P],
                                       x2_q[:, m, q * P:(q + 1) * P], ident, start=True, stop=True)
                mm.then_inc(residual_turned, 1)
                pe.wait_ge(y_split, n + 1)
                for q in range(QTILES):
                    for k in range(KC):
                        a = RW_AT + k * EXPERTS
                        mm = three(ps_qk[:, 0, q * EXPERTS:(q + 1) * EXPERTS],
                                   y_hi[:, k, q * P:(q + 1) * P], y_lo[:, k, q * P:(q + 1) * P],
                                   w_hi[:, a:a + EXPERTS], w_lo[:, a:a + EXPERTS], k == 0, k == KC - 1)
                mm.then_inc(routed, 1)
                for e in range(EXPERTS + 2):
                    if e < EXPERTS:
                        if e >= 2:
                            pe.wait_ge(hidden_ready, n * EXPERTS + (e - 1))
                        expand(e)
                    if e >= 2:
                        pe.wait_ge(hidden_split, n * EXPERTS + (e - 1))
                        if e >= 4:
                            pe.wait_ge(gated, n * EXPERTS + (e - 3))
                        contract(e - 2)

        @block.scalar
        def _(act):
            act.wait_ge(bias_zeroed, 1)
            for row in (0, 32):
                act.dma_start(bias_raw[row:row + 2, :, :], gate_bias).then_inc(bias_loaded, 16)
            nc.scalar.preload_act_table(ACT.Exp)
            act.wait_ge(gru_loaded, 64)
            act.wait_ge(consts_loaded, 64)

            with act.Fori(0, A_LOOPS) as i:
                for u in range(2):
                    t = i * 2 + u
                    act.wait_ge(gates_ready, t + 1)
                    nc.scalar.activation(rz[:, :], ps_o[:, u, CW:3 * CW], ACT.Tanh, scale=0.5).then_inc(rz_ready, 1)
                    act.wait_ge(cand_summed, t + 1)
                    nc.scalar.activation(cand[:, 2, :], cand[:, 1, :], ACT.Tanh).then_inc(cand_ready, 1)

            for m in range(KC):
                nc.scalar.activation(x2[:, m, :, :], xT[:, m, 0:STEPS, :].rearrange("p t b -> p b t"), ACT.Identity,
                                     bias=bo_s[:, m:m + 1]).then_inc(x2_updated, 2)

            def spread_k(j, half):
                act.wait_ge(qk_rotated, j * 4 + (2 * half + 2))
                for h in range(PER_GROUP):
                    rows = slice(HALF * h, HALF * (h + 1))
                    last = nc.scalar.copy(k_bd[rows, :, half * BH:(half + 1) * BH, h, :],
                                          k_s[rows, :, half * BH:(half + 1) * BH, :])
                last.then_inc(k_spread, 1)

            def exponent(g, half):
                act.wait_ge(shifted, g * 2 + (half + 1))
                nc.scalar.activation(prob[:, half, :, :], soft[:, half, :, :], ACT.Exp).then_inc(exp_ready, 1)

            def head_o(g, n):
                act.wait_ge(attended, g * 4 + (n + 1))
                half, hp = n // 2, n % 2
                nc.scalar.copy(o_hi[:, hp, half * TH:(half + 1) * TH], ps_o[:, hp, :]).then_inc(o_headed, 1)

            def take_v(j, par):
                for n in range(TILES // 2):
                    act.wait_ge(v_projected, j * 4 + (n + 1))
                    nc.scalar.copy(v_s[:, par, 2 * n:2 * n + 2, :], ps_o[:, n % 2, :]).then_inc(v_ready, 1)

            act.wait_ge(k_diag_zeroed, 1)
            take_v(0, 0)
            spread_k(0, 0)
            spread_k(0, 1)

            def group(g, par, last=False):
                exponent(g, 0)
                exponent(g, 1)
                if not last:
                    take_v(g + 1, 1 - par)
                    spread_k(g + 1, 0)
                for n in range(3):
                    head_o(g, n)
                if not last:
                    spread_k(g + 1, 1)
                head_o(g, 3)

            group(0, 0)
            with act.Fori(0, (GROUPS - 2) // 2) as i:
                for par in range(2):
                    group(i * 2 + (par + 1), 1 - par)
            group(GROUPS - 1, (GROUPS - 1) % 2, last=True)

            nc.scalar.preload_act_table(ACT.Silu)
            act.wait_ge(x2_updated, 4 * GROUPS + 4)
            nc.scalar.copy(x2_q, x2[:, :, 0:QB, :].rearrange("p m b t -> p m (b t)")).then_inc(quarter_copied, 1)

            def gate_output(n, e):
                if e == 0:
                    act.wait_ge(gates_summed, n + 1)
                act.wait_ge(contracted, n * EXPERTS + (e + 1))
                if e >= 2:
                    act.wait_ge(combined, n * EXPERTS + (e - 1))
                for q in range(QTILES):
                    last = nc.scalar.activation(gated_f[:, e % 2, q, :], ps_o[:, e % 2, q * DIM:(q + 1) * DIM], ACT.Copy,
                                                scale=pick[:, q, 2, e:e + 1])
                last.then_inc(gated, 1)

            def quarter(n, more):
                for m in range(KC):
                    act.wait_ge(conv_step[m], n * TAPS + TAPS)
                nc.scalar.copy(y_hi[:, :, :], y_f.rearrange("p m b t -> p m (b t)")).then_inc(y_headed, 1)
                act.wait_ge(residual_turned, n + 1)
                act.wait_ge(stored, n * 16 + 16)
                nc.scalar.copy(out_f, ps_qk[:, 1, :]).then_inc(residual_ready, 1)
                if more:
                    nc.scalar.copy(x2_q, x2[:, :, bass.ds(n * QB + QB, QB), :].rearrange("p m b t -> p m (b t)"))\
                        .then_inc(quarter_copied, 1)
                act.wait_ge(margin_ready, n + 1)
                nc.scalar.activation(route[:, :, 1:2], route[:, :, 0:1], ACT.Tanh, scale=0.5 / SPLIT).then_inc(odds_ready, 1)
                for e in range(EXPERTS + 2):
                    if e < EXPERTS:
                        act.wait_ge(expanded, n * EXPERTS + (e + 1))
                        if e >= 2:
                            act.wait_ge(hidden_ready, n * EXPERTS + (e - 1))
                        nc.scalar.activation(gate_f[:, e % 2, :], ps_s[:, e % 2, 0:QT], ACT.Silu, scale=1.0 / SPLIT)\
                            .then_inc(silu_ready, 1)
                    if 1 <= e <= EXPERTS:
                        act.wait_ge(hidden_ready, n * EXPERTS + e)
                        if e >= 3:
                            act.wait_ge(contracted, n * EXPERTS + (e - 2))
                        nc.scalar.copy(hid_hi[:, (e - 1) % 2, :], hid_f[:, (e - 1) % 2, :]).then_inc(hidden_headed, 1)
                    if e >= 2:
                        gate_output(n, e - 2)

            with act.Fori(0, QUARTERS - 1) as n:
                quarter(n, True)
            quarter(QUARTERS - 1, False)

        @block.vector
        def _(dve):
            nc.vector.memset(bias_raw[:, :, :], 0.0).then_inc(bias_zeroed, 1)
            nc.vector.memset(ones16[:, :], 1.0).then_inc(bias_ready, 1)
            nc.vector.memset(k_bd[:, 0, :, :, :], 0.0).then_inc(stored, 16)
            nc.vector.memset(k_bd[:, 1, :, :, :], 0.0).then_inc(k_diag_zeroed, 1)
            dve.wait_ge(bias_loaded, 32)
            nc.vector.tensor_copy(bias16[:, :, :], bias_raw[:, :, :]).then_inc(bias_ready, 1)
            dve.wait_ge(bias_ready, 2)
            nc.vector.tensor_tensor(bias16[32:64, :, :], bias_raw[32:64, :, :], bias16[32:64, :, :], ALU.subtract)\
                .then_inc(bias_ready, 1)
            dve.wait_ge(gru_loaded, 64)
            nc.vector.transpose(stateT[:, 1, :, :].rearrange("p e b -> p (e b)"), state[:, :]).then_inc(state_ready, 1)

            with dve.Fori(0, A_LOOPS) as i:
                for u in range(2):
                    t = i * 2 + u
                    r, z = rz[:, 0:CW], rz[:, CW:2 * CW]
                    dve.wait_ge(rz_ready, t + 1)
                    nc.vector.scalar_tensor_tensor(cand[:, 0, :], r, 1.0, ps_o[:, u, 3 * CW:4 * CW], ALU.add, ALU.mult)\
                        .then_inc(reset_done, 1)
                    nc.vector.tensor_scalar(blend[:, 0, :], z, -0.5, 0.5, ALU.mult, ALU.add)
                    dve.wait_ge(reset_done, t + 1)
                    nc.vector.scalar_tensor_tensor(cand[:, 1, :], cand[:, 0, :], 0.5, ps_o[:, u, 0:CW], ALU.mult, ALU.add)\
                        .then_inc(cand_summed, 1)
                    nc.vector.tensor_scalar(blend[:, 1, :], z, 0.5, 0.5, ALU.mult, ALU.add).then_inc(z_ready, 1)
                    dve.wait_ge(z_ready, t + 1)
                    nc.vector.tensor_tensor(blend[:, 2, :], blend[:, 1, :], state[:, :], ALU.mult).then_inc(blend_ready, 1)
                    dve.wait_ge(cand_ready, t + 1)
                    nc.vector.tensor_tensor(blend[:, 3, :], cand[:, 2, :], blend[:, 0, :], ALU.mult).then_inc(blend_ready, 1)
                    dve.wait_ge(blend_ready, t * 2 + 2)
                    nc.vector.tensor_tensor(state[:, :], blend[:, 3, :], blend[:, 2, :], ALU.add).then_inc(state_new, 1)
                    dve.wait_ge(hs_saved, t + 1)
                    dve.wait_ge(state_new, t + 1)
                    nc.vector.transpose(stateT[:, u, :, :].rearrange("p e b -> p (e b)"), state[:, :]).then_inc(state_ready, 1)

            def rotate(j, half, pair):
                n = 2 * half + pair
                dve.wait_ge(qk_projected, j * 4 + (n + 1))
                if isinstance(j, int) and j == 0:
                    if n >= 2:
                        dve.wait_ge(qk_rotated, n - 1)
                else:
                    dve.wait_ge(qk_rotated, j * 4 + (n - 1))
                cos, sin, neg = rot[3 * pair:3 * pair + 3]
                src = ps_qk[:, 2 * pair:2 * pair + 2, :].rearrange("p a (b t) -> p a b t", b=BH)
                into = prods[:, pair, :, :].rearrange("p n (a b t) -> p n a b t", a=2, b=BH)
                nc.vector.tensor_tensor(into[:, 0].rearrange("p a b t -> p (a b) t"), src.rearrange("p a b t -> p (a b) t"),
                                        over(cos, 2 * BH), ALU.mult)
                nc.vector.tensor_tensor(into[:, 1, 0], src[:, 1], over(neg, BH), ALU.mult)
                nc.vector.tensor_tensor(into[:, 1, 1], src[:, 0], over(sin, BH), ALU.mult).then_inc(qk_products, 1)

            rows = TILES_H * PER_GROUP

            def wide(a, half):
                return stats[:, half, a, :].rearrange("p (r o) -> p r o", o=1).broadcast_to([P, rows, STEPS])

            def softmax_front(g, half):
                dve.wait_ge(scored, g * 2 + (half + 1))
                nc.vector.tensor_tensor(soft[:, half, :, :], ps_s[:, half, :].rearrange("p (r t) -> p r t", t=STEPS),
                                        over(mask, rows), ALU.add).then_inc(masked, 1)
                dve.wait_ge(masked, g * 2 + (half + 1))
                nc.vector.tensor_reduce(stats[:, half, 0, :], soft[:, half, :, :], AX.X, ALU.max).then_inc(max_ready, 1)
                dve.wait_ge(max_ready, g * 2 + (half + 1))
                nc.vector.tensor_tensor(soft[:, half, :, :], soft[:, half, :, :], wide(0, half), ALU.subtract)\
                    .then_inc(shifted, 1)

            dve.wait_ge(pool_set, 1)

            def softmax_back(g, half):
                dve.wait_ge(exp_ready, g * 2 + (half + 1))
                nc.vector.tensor_reduce(stats[:, half, 1, :], prob[:, half, :, :], AX.X, ALU.add).then_inc(sum_ready, 1)
                dve.wait_ge(sum_ready, g * 2 + (half + 1))
                nc.vector.reciprocal(stats[:, half, 2, :], stats[:, half, 1, :]).then_inc(rsum_ready, 1)
                dve.wait_ge(rsum_ready, g * 2 + (half + 1))
                nc.vector.tensor_tensor(soft[:, half, :, :], prob[:, half, :, :], wide(2, half), ALU.mult)\
                    .then_inc(prob_ready, 1)
                dve.wait_ge(prob_ready, g * 2 + (half + 1))
                for b in range(TILE_B):
                    part = slice(STEPS * b, STEPS * (b + 1))
                    last = nc.vector.transpose(p_bd[part, half, :, STEPS * b:STEPS * (b + 1)], soft[part, half, :, :])
                last.then_inc(prob_turned, 1)

            def tail_o(g, n):
                half, hp = n // 2, n % 2
                dve.wait_ge(o_headed, g * 4 + (n + 1))
                cols = slice(half * TH, (half + 1) * TH)
                nc.vector.tensor_tensor(o_lo[:, hp, cols], ps_o[:, hp, :], o_hi[:, hp, cols], ALU.subtract)\
                    .then_inc(o_split, 1)

            def add_o(g):
                dve.wait_ge(x2_updated, g * 4 + 4)
                for m in range(KC):
                    for half in range(2):
                        dve.wait_ge(o_projected, g * 4 + (2 * m + half + 1))
                        part = x2[:, m, half * BH:(half + 1) * BH, :].rearrange("p b t -> p (b t)")
                        nc.vector.scalar_tensor_tensor(part, ps_qk[:, 2 * m + half, :], 1.0 / (SPLIT * SPLIT), part,
                                                       ALU.mult, ALU.add).then_inc(x2_updated, 1)

            dve.wait_ge(consts_loaded, 64)
            for half in range(2):
                for pair in range(2):
                    rotate(0, half, pair)
            def group(g, first=False, last=False):
                softmax_front(g, 0)
                softmax_front(g, 1)
                if not first:
                    add_o(g - 1)
                softmax_back(g, 0)
                if not last:
                    rotate(g + 1, 0, 0)
                    rotate(g + 1, 0, 1)
                softmax_back(g, 1)
                if not last:
                    rotate(g + 1, 1, 0)
                    rotate(g + 1, 1, 1)
                for n in range(4):
                    tail_o(g, n)

            group(0, first=True)
            with dve.Fori(1, GROUPS - 1) as g:
                group(g)
            group(GROUPS - 1, last=True)
            add_o(GROUPS - 1)

            x2_qv = x2_q.rearrange("p m (b t) -> p m b t", b=QB)

            def convolve(n, lags):
                for lag in lags:
                    for m in range(KC):
                        w = taps_s[:, m, TAPS - 1 - lag:TAPS - lag]
                        if lag == 0:
                            nc.vector.tensor_scalar(y_f[:, m], x2_qv[:, m], w, conv_bs[:, m:m + 1], ALU.mult, ALU.add)\
                                .then_inc(conv_step[m], 1)
                            continue
                        dve.wait_ge(conv_step[m], n * TAPS + lag)
                        nc.vector.scalar_tensor_tensor(y_f[:, m, :, lag:], x2_qv[:, m, :, 0:STEPS - lag], w,
                                                       y_f[:, m, :, lag:], ALU.mult, ALU.add).then_inc(conv_step[m], 1)

            def choose(n):
                dve.wait_ge(routed, n + 1)
                nc.vector.tensor_copy(logits[:, :, :], ps_qk[:, 0, 0:QTILES * EXPERTS].rearrange("p (q e) -> p q e", q=QTILES))
                dve.drain()
                for q in range(QTILES):
                    nc.vector.max(top[:, q, :], logits[:, q, :])
                dve.drain()
                for q in range(QTILES):
                    nc.vector.max_index(top_at[:, q, :], top[:, q, :], logits[:, q, :]).then_inc(top_found, 1)
                nc.vector.tensor_tensor(route[:, :, 0:1], top[:, :, 0:1], top[:, :, 1:2], ALU.subtract)\
                    .then_inc(margin_ready, 1)
                dve.wait_ge(top_found, n * QTILES + QTILES)
                nc.vector.tensor_copy(top_f[:, :, :], top_at[:, :, :]).then_inc(top_cast, 1)
                dve.wait_ge(odds_ready, n + 1)
                nc.vector.tensor_scalar(route[:, :, 2:3], route[:, :, 1:2], 0.5 / SPLIT, 0.5 / SPLIT, ALU.mult, ALU.add)
                nc.vector.tensor_scalar(route[:, :, 3:4], route[:, :, 1:2], -0.5 / SPLIT, 0.5 / SPLIT, ALU.mult, ALU.add)\
                    .then_inc(shares_ready, 1)
                dve.wait_ge(top_cast, n + 1)
                dve.wait_ge(shares_ready, n + 1)
                for q in range(QTILES):
                    for s in range(2):
                        last = nc.vector.tensor_scalar(pick[:, q, s, :], iota, top_f[:, q, s:s + 1], route[:, q, 2 + s:3 + s],
                                                       ALU.is_equal, ALU.mult)
                last.then_inc(picks_ready, 1)
                dve.wait_ge(picks_ready, n + 1)
                nc.vector.tensor_tensor(pick[:, :, 2, :], pick[:, :, 0, :], pick[:, :, 1, :], ALU.add).then_inc(gates_summed, 1)
                dve.wait_ge(gates_summed, n + 1)

            def hidden(n, e):
                dve.wait_ge(silu_ready, n * EXPERTS + (e + 1))
                if e >= 2:
                    dve.wait_ge(hidden_split, n * EXPERTS + (e - 1))
                nc.vector.scalar_tensor_tensor(hid_f[:, e % 2, :], ps_s[:, e % 2, QT:2 * QT], 1.0 / SPLIT,
                                               gate_f[:, e % 2, :], ALU.mult, ALU.mult).then_inc(hidden_ready, 1)

            def quarter(n, more):
                choose(n)
                for e in range(EXPERTS):
                    hidden(n, e)
                    if more:
                        if e == 0:
                            dve.wait_ge(quarter_copied, n + 2)
                            dve.wait_ge(y_split, n + 1)
                        convolve(n + 1, range(TAPS // EXPERTS * e, TAPS // EXPERTS * (e + 1)))

            dve.wait_ge(quarter_copied, 1)
            convolve(0, range(TAPS))
            with dve.Fori(0, QUARTERS - 1) as n:
                quarter(n, True)
            quarter(QUARTERS - 1, False)

        @block.gpsimd
        def _(pool):
            nc.gpsimd.memset(split_by[:, :], SPLIT).then_inc(hs_saved, 2)
            nc.gpsimd.memset(xT[:, :, STEPS:STEPS + 2, :], 0.0).then_inc(o_w_ready, 1)
            nc.gpsimd.memset(p_bd[:, :, :, :], 0.0).then_inc(pool_set, 1)
            pool.wait_ge(pool_set, 1)
            pool.wait_ge(gru_loaded, 64)
            for u in range(2):
                nc.gpsimd.tensor_copy(x_now[:, u, :, :], xT[:, :, u, :]).then_inc(x_ready, 1)
            pool.wait_ge(first_loaded, 16)
            with pool.Fori(0, A_LOOPS) as i:
                cols = bass.ds(i * SPLIT_STEP, SPLIT_STEP)
                for u in range(2):
                    t = i * 2 + u
                    now = bass.ds(t, 1)
                    pool.wait_ge(x_projected, t + 1)
                    nc.gpsimd.tensor_copy(x_now[:, u, :, :], xT[:, :, bass.ds(t + 2, 1), :].rearrange("p k o b -> p k (o b)"))\
                        .then_inc(x_ready, 1)
                    pool.wait_ge(state_ready, t + 2)
                    hi = hs_hi[:, :, :, now].rearrange("p k b o -> p k (b o)")
                    lo = hs_lo[:, :, :, now].rearrange("p k b o -> p k (b o)")
                    nc.gpsimd.tensor_copy(hi, stateT[:, u, :, :]).then_inc(hs_hi_saved, 1)
                    if u == 0:
                        nc.gpsimd.tensor_tensor(arena[:, cols], arena[:, cols],
                                                split_by[:, 0:1].broadcast_to([P, SPLIT_STEP]), ALU.mult).then_inc(w_scaled, 1)
                    pool.wait_ge(hs_hi_saved, t + 1)
                    nc.gpsimd.tensor_tensor(lo, stateT[:, u, :, :], hi, ALU.subtract).then_inc(hs_saved, 1)
                    if u == 0:
                        pool.wait_ge(w_scaled, i + 1)
                        nc.gpsimd.tensor_copy(w_hi[:, cols], arena[:, cols]).then_inc(w_headed, 1)
                    else:
                        pool.wait_ge(w_headed, i + 1)
                        nc.gpsimd.tensor_tensor(w_lo[:, cols], arena[:, cols], w_hi[:, cols], ALU.subtract)\
                            .then_inc(w_split, 1)

            def add_products(j, half, pair):
                n = 2 * half + pair
                pool.wait_ge(qk_products, j * 4 + (n + 1))
                into = (q_s, k_s)[pair][:, :, half * BH:(half + 1) * BH, :].rearrange("p a b t -> p a (b t)")
                both = prods[:, pair, :, :].rearrange("p n (a c) -> p n a c", a=2)
                nc.gpsimd.tensor_tensor(into, both[:, 0], both[:, 1], ALU.add).then_inc(qk_rotated, 1)

            qkv_view = raw_qkv[:, :].rearrange("p (k c) -> p k c", k=KC)

            def split_part(w, lo, hi):
                return w[:, QKV_AT:QKV_AT + QKV_COLS].rearrange("p (k c) -> p k c", k=KC)[:, :, lo:hi]

            def split_cols(raw, head, tail, order, ready):
                by = split_by[:, 0:1]
                by = by.broadcast_to([P, raw.shape[1]]) if len(raw.shape) == 2 else \
                    by.rearrange("p (o c) -> p o c", o=1).broadcast_to([P, raw.shape[1], raw.shape[2]])
                nc.gpsimd.tensor_tensor(head, raw, by, ALU.mult).then_inc(w_headed, 1)
                pool.wait_ge(w_headed, order)
                nc.gpsimd.tensor_tensor(raw, raw, by, ALU.mult).then_inc(w_scaled, 1)
                pool.wait_ge(w_scaled, order)
                nc.gpsimd.tensor_tensor(tail, raw, head, ALU.subtract).then_inc(ready, 1)

            def split_v(j, order):
                pool.wait_ge(qkv_loaded, j * 16)
                pool.wait_ge(v_projected, j * 4)
                split_cols(qkv_view[:, :, 2 * DIM:], split_part(w_hi, 2 * DIM, 3 * DIM), split_part(w_lo, 2 * DIM, 3 * DIM),
                           order, v_w_ready)

            def split_qk(j, order):
                pool.wait_ge(qk_projected, j * 4)
                split_cols(qkv_view[:, :, 0:2 * DIM], split_part(w_hi, 0, 2 * DIM), split_part(w_lo, 0, 2 * DIM), order,
                           qk_w_ready)

            def split_o(j, order):
                pool.wait_ge(o_loaded, j * 16)
                pool.wait_ge(o_projected, j * 4)
                split_cols(raw_o[:, :], w_hi[:, WO_AT:WO_AT + WO_COLS], w_lo[:, WO_AT:WO_AT + WO_COLS], order, o_w_ready)

            def products(j, half):
                for pair in range(2):
                    add_products(j, half, pair)

            def group(g, order, first=False, last=False):
                if not first:
                    split_o(g, order)
                products(g + 1, 0)
                if not last:
                    split_v(g + 2, order + (0 if first else 1))
                products(g + 1, 1)
                if not last:
                    split_qk(g + 2, order + (1 if first else 2))

            products(0, 0)
            split_v(1, A_LOOPS + 1)
            products(0, 1)
            split_qk(1, A_LOOPS + 2)
            group(0, A_LOOPS + 3, first=True)
            with pool.Fori(1, GROUPS - 2) as g:
                group(g, g * 3 + (A_LOOPS + 2))
            order = 3 * (GROUPS - 2) + A_LOOPS + 2
            group(GROUPS - 2, order, last=True)
            split_o(GROUPS - 1, order + 1)

            def quarter(n):
                pool.wait_ge(y_headed, n + 1)
                nc.gpsimd.tensor_tensor(y_lo[:, :, :], y_f.rearrange("p m b t -> p m (b t)"), y_hi[:, :, :], ALU.subtract)\
                    .then_inc(y_split, 1)
                def combine(e):
                    pool.wait_ge(gated, n * EXPERTS + (e + 1))
                    if e == 0:
                        pool.wait_ge(residual_ready, n + 1)
                    else:
                        pool.wait_ge(combined, n * EXPERTS + e)
                    nc.gpsimd.tensor_tensor(out_f, out_f, gated_f[:, e % 2, :, :], ALU.add).then_inc(combined, 1)

                for e in range(EXPERTS):
                    if e >= 3:
                        combine(e - 3)
                    pool.wait_ge(hidden_headed, n * EXPERTS + (e + 1))
                    nc.gpsimd.tensor_tensor(hid_lo[:, e % 2, :], hid_f[:, e % 2, :], hid_hi[:, e % 2, :], ALU.subtract)\
                        .then_inc(hidden_split, 1)
                for e in range(EXPERTS - 3, EXPERTS):
                    combine(e)

            with pool.Fori(0, QUARTERS) as n:
                quarter(n)


def _tables(np):
    inv = (1.0 / 10000.0 ** (np.arange(0, HEAD_DIM, 2, dtype=np.float32) / np.float32(HEAD_DIM))).astype(np.float32)
    angle = (np.arange(STEPS, dtype=np.float32)[None, :] * inv[:, None]).astype(np.float32)
    cos, sin = np.cos(angle).astype(np.float32), np.sin(angle).astype(np.float32)
    t = np.zeros((P, TAB_COLS), np.float32)
    for pair, scale in enumerate((HEAD_DIM ** -0.5 / SPLIT, 1.0 / SPLIT)):
        for n, table in enumerate((cos, sin, -sin)):
            at = (3 * pair + n) * STEPS
            t[:, at:at + STEPS] = np.tile(table * np.float32(scale), (P // HALF, 1))
    q, k = np.arange(P)[:, None] % STEPS, np.arange(STEPS)[None, :]
    t[:, TAB_MASK:TAB_MASK + STEPS] = np.where(q >= k, 0.0, -1e30)
    t[:, TAB_IDENT:TAB_IDENT + P] = np.eye(P)
    t[:, TAB_IOTA:] = np.arange(EXPERTS)
    return t


def kernel(**inputs):
    import numpy as np
    import concourse.bacc as _bacc
    from concourse.bass_utils import run_bass_kernel_spmd as _run

    a = {n: np.asarray(v) for n, v in inputs.items()}
    con = np.ascontiguousarray

    x_t = con(a["x"].transpose(2, 1, 0).reshape(KC, P, STEPS, BATCH).transpose(1, 0, 2, 3))
    h0 = con(a["cond_2048"].reshape(BATCH, CB, CW).transpose(1, 0, 2).reshape(P, CW))
    w_ih = con(a["L0_cond_W_ih"].reshape(KC, P, 3, CB, CW).transpose(1, 0, 3, 2, 4)[:, :, :, [2, 0, 1]]
               .reshape(P, KC, CB, 3 * CW))

    def state_rows(w):
        return w.reshape(CB, KC, 32, -1).transpose(0, 2, 1, 3).reshape(P, KC, -1)

    w_hh = con(state_rows(a["L0_cond_W_hh"]).reshape(P, KC, 3, CB, CW).transpose(0, 1, 3, 2, 4)
               .reshape(P, KC, CB, 3 * CW))
    bi, bh = (a[n].reshape(3, CB, CW) for n in ("L0_cond_b_ih", "L0_cond_b_hh"))
    gate_bias = np.zeros((2, CB, 4 * CW), np.float32)
    for n, g in enumerate((2, 0, 1)):
        gate_bias[0, :, n * CW:(n + 1) * CW] = bi[g]
    for n, g in enumerate((0, 1, 2)):
        gate_bias[1, :, (n + 1) * CW:(n + 2) * CW] = bh[g]

    def rotary_rows(w):
        return w.reshape(GROUPS, PER_GROUP, 2, HALF, DIM).transpose(0, 2, 1, 3, 4).reshape(GROUPS, DIM, DIM)

    qkv = np.stack([rotary_rows(a["L0_attn_Wq"]), rotary_rows(a["L0_attn_Wk"]),
                    a["L0_attn_Wv"].reshape(GROUPS, VW, DIM)], 1)
    qkv = qkv.transpose(0, 3, 1, 2)
    qkv = con(np.stack([state_rows(w) for w in qkv]).reshape(GROUPS, P, QKV_COLS))
    w_o = con(a["L0_attn_Wo"].T.reshape(GROUPS, HP, P, DIM).transpose(0, 2, 1, 3).reshape(GROUPS, P, WO_COLS))

    def up(w):
        return w.reshape(EXPERTS, KC, P, FF).transpose(2, 0, 1, 3).reshape(P, W1_COLS)

    w_first = con(np.concatenate([
        up(a["L0_ffn_w1"]), up(a["L0_ffn_w2"]), a["L0_ffn_w3"].transpose(1, 0, 2).reshape(P, W3_COLS),
        qkv[0], w_o[0], a["L0_ffn_router_w"].T.reshape(KC, P, EXPERTS).transpose(1, 0, 2).reshape(P, RW_COLS)], 1))
    arrays = {
        "x_t": x_t, "h0": h0, "w_ih": w_ih, "w_hh": w_hh, "gate_bias": gate_bias, "w_first": w_first,
        "w_qkv": con(qkv[1:]), "w_o": con(w_o[1:]),
        "bo": con(a["L0_attn_bo"].reshape(KC, P).T), "tables": _tables(np),
        "taps": con(a["cond_2048"].T.reshape(KC, P, TAPS).transpose(1, 0, 2)),
        "conv_b": con(a["L0_cond2_b"].reshape(KC, P).T),
    }
    nc = _bacc.Bacc("TRN2", target_bir_lowering=False, num_devices=1)
    args = [nc.dram_tensor(f"{n}_dram", v.shape, mybir.dt.from_np(v.dtype), kind="ExternalInput").ap()
            for n, v in arrays.items()]
    out = nc.dram_tensor("out_dram", (QUARTERS, QTILES, P, DIM), F32, kind="ExternalOutput").ap()
    block_kernel(nc, *args, out)
    r = _run(nc, [{f"{n}_dram": v for n, v in arrays.items()}], core_ids=[0])
    return r.results[0]["out_dram"].reshape(BATCH, STEPS, DIM)
```

```python
from contextlib import ExitStack

import concourse.bass as bass
from concourse import mybir

F32 = mybir.dt.float32
F16 = mybir.dt.float16
U32 = mybir.dt.uint32
ALU = mybir.AluOpType
ACT = mybir.ActivationFunctionType
AX = mybir.AxisListType

P = 128
BATCH, STEPS, DIM = 32, 32, 256
TOKENS = BATCH * STEPS
KC = DIM // P
HEADS, HEAD_DIM = 32, 64
HALF = HEAD_DIM // 2
PER_GROUP = P // HALF
GROUPS = HEADS // PER_GROUP
CB = 4
CW = DIM // CB
TILE_B = P // STEPS
TILES = TOKENS // P
BH = BATCH // 2
TH = TOKENS // 2
TILES_H = TILES // 2
HP = PER_GROUP // 2
VW = PER_GROUP * HEAD_DIM
EXPERTS, FF = 8, 128
CH_GROUPS = DIM // CB
QUARTERS = 4
QB = BATCH // QUARTERS
QT = TOKENS // QUARTERS
QTILES = QT // P
HALF_FIRST = ((0, 0), (0, 1), (1, 0), (1, 1))
CHUNK_FIRST = ((0, 0), (1, 0), (0, 1), (1, 1))
SPLIT = 256.0

QK_COLS = KC * 2 * DIM
V_COLS = KC * VW
WO_COLS = HP * DIM
W1_COLS = EXPERTS * KC * FF
W3_COLS = EXPERTS * DIM
RW_COLS = KC * EXPERTS
QK_AT = 0
QK1_AT = QK_AT + QK_COLS
V_AT = QK1_AT + QK_COLS
WO_AT = V_AT + V_COLS
RW_AT = WO_AT + WO_COLS
W1_AT = RW_AT + RW_COLS
W2_AT = W1_AT + W1_COLS
W3_AT = W2_AT + W1_COLS
USED_COLS = W3_AT + W3_COLS
A_LOOPS = STEPS // 2
A_HALF = A_LOOPS // 2
A_SPLIT, A_SPLIT_2, A_SPLIT_END = 3, 9, A_LOOPS - 2
SPLITS = A_SPLIT_END - A_SPLIT
SPLIT_STEP = -(-USED_COLS // SPLITS)
SPLIT_COLS = SPLIT_STEP * SPLITS
CHUNK = STEPS // A_HALF
X_FIRST = 2 * A_SPLIT + 2
WARM = 24
KEEP = 11
KEEP_C = 5

ROT = 6
TAB_MASK = ROT * STEPS
TAB_IDENT = TAB_MASK + STEPS
TAB_IOTA = TAB_IDENT + P
TAB_COLS = TAB_IOTA + EXPERTS


def block_kernel(nc: bass.Bass, x_t, h0, w_ih, w_hh, gate_bias, w_first, w_qk, w_v, w_o, bo, tables, w_conv, conv_b, out):
    ctx = ExitStack()
    with ctx:
        def sb(name, shape, dt=F32):
            return ctx.enter_context(nc.sbuf_tensor(name, shape, dt))

        def pb(name, shape):
            return ctx.enter_context(nc.psum_tensor(name, shape, F32))

        def sem(name):
            return ctx.enter_context(nc.semaphore(name))

        ps_s = pb("ps_s", [P, 2, 512])
        ps_qk = pb("ps_qk", [P, 4, 512])
        ps_o = pb("ps_o", [P, 2, 512])

        xT = sb("xT", [P, KC, STEPS + 2, BATCH])
        x2 = sb("x2", [P, KC, BATCH, STEPS])
        hs_hi = sb("hs_hi", [P, KC, BATCH, STEPS], F16)
        hs_lo = sb("hs_lo", [P, KC, BATCH, STEPS], F16)
        w_gru = sb("w_gru", [P, 2, KC, CB, 3 * CW])
        wih, whh = w_gru[:, 0], w_gru[:, 1]
        bias_raw = sb("bias_raw", [P, 2, 4 * CW])
        bias16 = sb("bias16", [P, 4 * CW], F16)
        ones16 = sb("ones16", [P, P], F16)
        warm = sb("warm", [P, 512], F16)
        x_now = sb("x_now", [P, 2, KC, BATCH])
        state = sb("state", [P, CW])
        stateT = sb("stateT", [P, 2, KC, BATCH])
        reset = sb("reset", [P, CW])
        update = sb("update", [P, CW])
        cand = sb("cand", [P, 2, CW])
        blend = sb("blend", [P, 3, CW])
        arena = sb("arena", [P, SPLIT_COLS])
        w_hi = sb("w_hi", [P, SPLIT_COLS], F16)
        w_lo = sb("w_lo", [P, SPLIT_COLS], F16)
        split_by = sb("split_by", [P, 1])
        raw_qk = sb("raw_qk", [P, QK_COLS])
        raw_v = sb("raw_v", [P, V_COLS])
        raw_o = sb("raw_o", [P, WO_COLS])
        tab = sb("tab", [P, TAB_COLS])
        bo_s = sb("bo_s", [P, KC])
        conv_bs = sb("conv_bs", [P, KC])
        k_bd = sb("k_bd", [P, 2, BATCH, PER_GROUP, STEPS])
        v_s = sb("v_s", [P, TILES, VW])
        soft = sb("soft", [P, 2, TILES_H * PER_GROUP, STEPS])
        prob = sb("prob", [P, 2, TILES_H * PER_GROUP, STEPS])
        stats = sb("stats", [P, 2, 3, TILES_H * PER_GROUP])
        p_bd = sb("p_bd", [P, 2, TILES_H * PER_GROUP, P])
        o_hi = sb("o_hi", [P, HP, TOKENS], F16)
        o_lo = sb("o_lo", [P, HP, TOKENS], F16)

        qk_cols = 2 * TOKENS
        q_s = arena[:, 0:qk_cols].rearrange("p (a b t) -> p a b t", a=2, b=BATCH)
        k_s = arena[:, qk_cols:2 * qk_cols].rearrange("p (a b t) -> p a b t", a=2, b=BATCH)
        prods = arena[:, 2 * qk_cols:4 * qk_cols].rearrange("p (u n c) -> p u n c", u=2, n=2)
        conv_raw = w_gru[:, :, :, :, :].rearrange("p a k c g -> p (a k c g)")[:, 0:CH_GROUPS * STEPS]\
            .rearrange("p (g t) -> p g t", g=CH_GROUPS)
        q_raw = w_gru[:, :, :, :, :].rearrange("p a k c g -> p (a k c g)")[:, CH_GROUPS * STEPS:CH_GROUPS * STEPS + TOKENS]\
            .rearrange("p (a b t) -> p a b t", a=2, b=BH)
        conv_w = xT[:, :, :, :].rearrange("p k t b -> p (k t b)")[:, 0:CH_GROUPS * STEPS].bitcast(F16)\
            .rearrange("p (g t n) -> p g t n", g=CH_GROUPS, n=2)
        conv_bd = k_bd[:, :, :, :, :].rearrange("p a b h t -> p (a b h t)").bitcast(F16)\
            .rearrange("p (g c t n) -> p g c t n", g=CH_GROUPS, c=CB, n=2)
        x_turned_f = arena[:, 0:qk_cols].rearrange("p (m b c) -> p m b c", m=KC, b=BATCH)
        y_turned_f = arena[:, qk_cols:2 * qk_cols].rearrange("p (m b t) -> p m b t", m=KC, b=BATCH)
        out_f = arena[:, 2 * qk_cols:3 * qk_cols].rearrange("p (n c) -> p n c", n=TILES)
        at = 3 * qk_cols
        gate_f = arena[:, at:at + 2 * QT].rearrange("p (u c) -> p u c", u=2)
        hid_f = arena[:, at + 2 * QT:at + 4 * QT].rearrange("p (u c) -> p u c", u=2)
        xc_hi = hs_hi[:, :, :, :].rearrange("p m a b -> p m (a b)")
        xc_lo = hs_lo[:, :, :, :].rearrange("p m a b -> p m (a b)")
        y_hi, y_lo = o_hi, o_lo
        hid_hi = sb("hid_hi", [P, 2, QT], F16)
        hid_lo = sb("hid_lo", [P, 2, QT], F16)
        logits = sb("logits", [P, TILES, EXPERTS])
        top = sb("top", [P, TILES, 8])
        top_at = sb("top_at", [P, TILES, 8], U32)
        top_f = sb("top_f", [P, TILES, 8])
        route = sb("route", [P, TILES, 4])
        pick = sb("pick", [P, TILES, 3, EXPERTS])

        rot = [tab[:, n * STEPS:(n + 1) * STEPS] for n in range(ROT)]
        mask = tab[:, TAB_MASK:TAB_MASK + STEPS]
        ident = tab[:, TAB_IDENT:TAB_IDENT + P]
        iota = tab[:, TAB_IOTA:TAB_IOTA + EXPERTS]

        def qk_w(w, at, pair, k):
            a = at + (k * 2 + pair) * DIM
            return w[:, a:a + DIM]

        def v_w(w, k):
            return w[:, V_AT + k * VW:V_AT + (k + 1) * VW]

        def over(table, n):
            return table.rearrange("p (o t) -> p o t", o=1).broadcast_to([P, n, STEPS])

        gru_loaded = sem("gru_loaded")
        bias_loaded = sem("bias_loaded")
        x_loaded = sem("x_loaded")
        first_loaded = [sem(f"first_loaded{part}") for part in range(2)]
        consts_loaded = sem("consts_loaded")
        qk_loaded = sem("qk_loaded")
        v_loaded = sem("v_loaded")
        o_loaded = sem("o_loaded")
        warm_ready = sem("warm_ready")
        bias_ready = sem("bias_ready")
        k_diag_zeroed = sem("k_diag_zeroed")
        pool_set = sem("pool_set")
        x_ready = sem("x_ready")
        x_projected = sem("x_projected")
        reset_gates = sem("reset_gates")
        update_gates = sem("update_gates")
        reset_ready = sem("reset_ready")
        update_ready = sem("update_ready")
        reset_done = sem("reset_done")
        cand_summed = sem("cand_summed")
        cand_ready = sem("cand_ready")
        blend_ready = sem("blend_ready")
        state_new = sem("state_new")
        state_ready = sem("state_ready")
        hs_hi_saved = sem("hs_hi_saved")
        hs_saved = sem("hs_saved")
        w_scaled = sem("w_scaled")
        w_headed = sem("w_headed")
        w_split = sem("w_split")
        x2_updated = sem("x2_updated")
        qk_projected = sem("qk_projected")
        qk_products = sem("qk_products")
        qk_rotated = sem("qk_rotated")
        k_spread = sem("k_spread")
        qk_w_ready = sem("qk_w_ready")
        v_w_ready = sem("v_w_ready")
        o_w_ready = sem("o_w_ready")
        v_projected = sem("v_projected")
        v_ready = sem("v_ready")
        scored = sem("scored")
        masked = sem("masked")
        max_ready = sem("max_ready")
        shifted = sem("shifted")
        exp_ready = sem("exp_ready")
        sum_ready = sem("sum_ready")
        rsum_ready = sem("rsum_ready")
        prob_ready = sem("prob_ready")
        prob_turned = sem("prob_turned")
        attended = sem("attended")
        o_headed = sem("o_headed")
        o_split = sem("o_split")
        o_projected = sem("o_projected")
        conv_loaded = sem("conv_loaded")
        conv_w_headed = sem("conv_w_headed")
        conv_w_split = sem("conv_w_split")
        conv_bd_dve = sem("conv_bd_dve")
        conv_bd_pool = sem("conv_bd_pool")
        conv_bd_act = sem("conv_bd_act")
        q_taken = sem("q_taken")
        q_multiplied = sem("q_multiplied")
        x_turned = sem("x_turned")
        x_headed = sem("x_headed")
        x_split = sem("x_split")
        convolved = sem("convolved")
        y_turned = sem("y_turned")
        y_headed = sem("y_headed")
        y_split = sem("y_split")
        routed = sem("routed")
        residual_turned = sem("residual_turned")
        residual_ready = sem("residual_ready")
        top_found = sem("top_found")
        top_cast = sem("top_cast")
        margin_ready = sem("margin_ready")
        odds_ready = sem("odds_ready")
        shares_ready = sem("shares_ready")
        places_found = sem("places_found")
        picks_ready = sem("picks_ready")
        gates_summed = sem("gates_summed")
        expanded = sem("expanded")
        silu_ready = sem("silu_ready")
        hidden_ready = sem("hidden_ready")
        hidden_headed = sem("hidden_headed")
        hidden_split = sem("hidden_split")
        contracted = sem("contracted")
        combined = sem("combined")
        stored = sem("stored")

        block = ctx.enter_context(nc.Block())

        @block.sync
        def _(sp):
            sp.dma_start(state[:, :], h0).then_inc(gru_loaded, 16)
            sp.dma_start(xT[:, :, 0:X_FIRST, :], x_t[:, :, 0:X_FIRST, :]).then_inc(gru_loaded, 16)
            sp.dma_start(wih, w_ih).then_inc(gru_loaded, 16)
            sp.dma_start(whh, w_hh).then_inc(gru_loaded, 16)
            sp.dma_start(xT[:, :, X_FIRST:STEPS, :], x_t[:, :, X_FIRST:STEPS, :]).then_inc(x_loaded, 16)
            for part in range(2):
                cut = (A_SPLIT_2 - A_SPLIT) * SPLIT_STEP
                cols = slice(cut) if part == 0 else slice(cut, SPLIT_COLS)
                sp.dma_start(arena[:, cols], w_first[:, cols]).then_inc(first_loaded[part], 16)
            sp.dma_start(tab[:, :], tables).then_inc(consts_loaded, 16)
            sp.dma_start(conv_bs[:, :], conv_b).then_inc(consts_loaded, 16)
            sp.dma_start(bo_s[:, :], bo).then_inc(consts_loaded, 16)
            def load(raw, w, at, loaded):
                sp.dma_start(raw[:, :], w[bass.ds(at, 1)].rearrange("o p c -> p (o c)")).then_inc(loaded, 16)

            load(raw_qk, w_qk, 0, qk_loaded)
            load(raw_v, w_v, 0, v_loaded)
            load(raw_o, w_o, 0, o_loaded)
            sp.wait_ge(update_gates, STEPS)
            sp.dma_start(conv_raw, w_conv).then_inc(conv_loaded, 16)
            with sp.Fori(1, GROUPS - 2) as j:
                sp.wait_ge(qk_w_ready, j)
                load(raw_qk, w_qk, j, qk_loaded)
                sp.wait_ge(v_w_ready, j)
                load(raw_v, w_v, j, v_loaded)
                sp.wait_ge(o_w_ready, j + 1)
                load(raw_o, w_o, j, o_loaded)
            sp.wait_ge(v_w_ready, GROUPS - 2)
            load(raw_v, w_v, GROUPS - 2, v_loaded)
            sp.wait_ge(o_w_ready, GROUPS - 1)
            load(raw_o, w_o, GROUPS - 2, o_loaded)
            with sp.Fori(0, QUARTERS) as n:
                sp.wait_ge(combined, n * EXPERTS + EXPERTS)
                sp.dma_start(out[bass.ds(n, 1)].rearrange("o q p c -> p (o q) c"), out_f[:, bass.ds(n * QTILES, QTILES), :])\
                    .then_inc(stored, 16)
            sp.wait_ge(stored, 16 * QUARTERS)

        @block.tensor
        def _(pe):
            def three(ps, a_hi, a_lo, b_hi, b_lo, first, last):
                pe.matmul(ps, a_lo, b_hi, start=first, stop=False)
                pe.matmul(ps, a_hi, b_lo, start=False, stop=False)
                return pe.matmul(ps, a_hi, b_hi, start=False, stop=last)

            def gru_step(t, u):
                pe.matmul(ps_o[:, u, 0:3 * CW], ones16[:, :], bias16[:, 0:3 * CW], start=True, stop=False, skip_group_check=True)
                pe.matmul(ps_s[:, u, 0:CW], ones16[:, :], bias16[:, 3 * CW:4 * CW], start=True, stop=False, skip_group_check=True)
                pe.wait_ge(x_ready, t + 1)
                for bank, cols, w_cols in ((ps_o, slice(0, 2 * CW), slice(0, 2 * CW)), (ps_s, slice(0, CW), slice(2 * CW, 3 * CW))):
                    for k in range(KC):
                        for c in range(CB):
                            mm = pe.matmul(bank[BATCH * c:BATCH * (c + 1), u, cols], x_now[:, u, k, :], wih[:, k, c, w_cols],
                                           start=False, stop=False, skip_group_check=True)
                mm.then_inc(x_projected, 1)
                pe.wait_ge(state_ready, t + 1)
                for bank, cols, w_cols, ready in ((ps_o, slice(CW, 3 * CW), slice(0, 2 * CW), reset_gates),
                                                  (ps_s, slice(0, CW), slice(2 * CW, 3 * CW), update_gates)):
                    for k in range(KC):
                        for c in range(CB):
                            mm = pe.matmul(bank[BATCH * c:BATCH * (c + 1), u, cols], stateT[:, 1 - u, k, :],
                                           whh[:, k, c, w_cols], start=False, stop=(k == KC - 1), skip_group_check=True)
                    mm.then_inc(ready, 1)

            def project_chunk(chunk, pair):
                steps = bass.ds(chunk * CHUNK, CHUNK)
                pe.wait_ge(hs_saved, chunk * CHUNK + (CHUNK + 2))
                for part in range(2):
                    cols = slice(part * P, part * P + P)
                    for k in range(KC):
                        mm = three(ps_qk[:, 2 * pair + part, :].rearrange("p (b t) -> p b t", b=BH)[:, :, steps],
                                   qk_w(w_hi, QK_AT, pair, k)[:, cols], qk_w(w_lo, QK_AT, pair, k)[:, cols],
                                   hs_hi[:, k, 0:BH, steps], hs_lo[:, k, 0:BH, steps], k == 0, k == KC - 1)
                return mm

            def keep_clock(products, bank):
                for n in range(products):
                    pe.matmul(bank, warm[:, 0:P], warm[:, :], start=True, stop=True)

            pe.wait_ge(warm_ready, 1)
            keep_clock(WARM, ps_qk[:, 0, :])
            pe.wait_ge(gru_loaded, 64)
            pe.wait_ge(bias_ready, 4)
            with pe.Fori(0, A_HALF) as i:
                for u in range(2):
                    gru_step(i * 2 + u, u)
            pe.wait_ge(w_split, -(-QK_COLS // SPLIT_STEP))
            with pe.Fori(0, A_HALF - 1) as i:
                for u in range(2):
                    gru_step(i * 2 + (STEPS // 2 + u), u)
                    project_chunk(i, u)
            for u in range(2):
                gru_step(STEPS - 2 + u, u)
            keep_clock(KEEP, ps_s[:, 0, :])
            for pair in range(2):
                project_chunk(A_HALF - 1, pair).then_inc(qk_projected, 1)

            def project_qk(j, half):
                at = QK1_AT if isinstance(j, int) and j == 1 else QK_AT
                for pair in range(2):
                    if isinstance(j, int) and (j, half, pair) == (1, 1, 1):
                        pe.wait_ge(q_taken, 1)
                    elif half == 1 or (isinstance(j, int) and j == 1):
                        pe.wait_ge(qk_products, j * 4 + (2 * half + pair - 1))
                    for part in range(2):
                        for k in range(KC):
                            cols = slice(part * P, part * P + P)
                            mm = three(ps_qk[:, 2 * pair + part, :],
                                       qk_w(w_hi, at, pair, k)[:, cols], qk_w(w_lo, at, pair, k)[:, cols],
                                       hs_hi[:, k, half * BH:(half + 1) * BH, :], hs_lo[:, k, half * BH:(half + 1) * BH, :],
                                       k == 0, k == KC - 1)
                    mm.then_inc(qk_projected, 1)

            def project_v(j, pairs=range(TILES // 2)):
                for n in pairs:
                    if n >= 2:
                        pe.wait_ge(v_ready, j * 4 + (n - 1))
                    elif not (isinstance(j, int) and j == 0):
                        pe.wait_ge(o_split, j * 4 + (n - 1))
                    for h in range(2):
                        tile = 2 * n + h
                        seqs = slice(tile * TILE_B, (tile + 1) * TILE_B)
                        for k in range(KC):
                            mm = three(ps_o[:, n % 2, h * VW:(h + 1) * VW],
                                       hs_hi[:, k, seqs, :], hs_lo[:, k, seqs, :],
                                       v_w(w_hi, k), v_w(w_lo, k), k == 0, k == KC - 1)
                    mm.then_inc(v_projected, 1)

            def score(g, half):
                pe.wait_ge(k_spread, g * 2 + (half + 1))
                pe.wait_ge(qk_rotated, g * 4 + (2 * half + 2))
                for tile in range(TILES_H):
                    for part in range(2):
                        for b in range(TILE_B):
                            seq = half * BH + tile * TILE_B + b
                            mm = pe.matmul(ps_s[STEPS * b:STEPS * (b + 1), half, tile * P:(tile + 1) * P],
                                           q_s[:, part, seq, :], k_bd[:, part, seq, :, :],
                                           start=(part == 0), stop=(part == 1), skip_group_check=True)
                mm.then_inc(scored, 1)

            def attend(g, half):
                pe.wait_ge(prob_turned, g * 2 + (half + 1))
                if half == 0:
                    pe.wait_ge(v_ready, g * 4 + 4)
                for hp in range(HP):
                    if half == 1:
                        pe.wait_ge(o_split, g * 4 + (hp + 1))
                    for tile in range(TILES_H):
                        for e in range(2):
                            head = 2 * hp + e
                            mm = pe.matmul(ps_o[HEAD_DIM * e:HEAD_DIM * (e + 1), hp, tile * P:(tile + 1) * P],
                                           v_s[:, half * TILES_H + tile, head * HEAD_DIM:(head + 1) * HEAD_DIM],
                                           p_bd[:, half, tile * PER_GROUP + head, :], start=True, stop=True,
                                           skip_group_check=True)
                    mm.then_inc(attended, 1)

            def project_o(g, order):
                pe.wait_ge(o_w_ready, g + 1)
                for half, m in order:
                    if m == 0:
                        pe.wait_ge(o_split, g * 4 + (2 * half + 2))
                    for hp in range(HP):
                        at = WO_AT + hp * DIM + m * P
                        mm = three(ps_qk[:, 2 * m + half, :], w_hi[:, at:at + P], w_lo[:, at:at + P],
                                   o_hi[:, hp, half * TH:(half + 1) * TH], o_lo[:, hp, half * TH:(half + 1) * TH],
                                   hp == 0, hp == HP - 1)
                    mm.then_inc(o_projected, 1)

            def group(g, scores=True, projections=True):
                attend(g, 0)
                if scores:
                    score(g + 1, 0)
                attend(g, 1)
                if scores:
                    pe.wait_ge(qk_products, g * 4 + 8)
                    pe.wait_ge(q_taken, 2)
                project_o(g, HALF_FIRST if scores else CHUNK_FIRST)
                if scores:
                    score(g + 1, 1)
                if projections:
                    pe.wait_ge(qk_w_ready, g + 1)
                    pe.wait_ge(x2_updated, g * 4 + 8)
                    project_qk(g + 2, 0)
                if scores:
                    pe.wait_ge(v_w_ready, g + 1)
                    project_v(g + 1)
                if projections:
                    project_qk(g + 2, 1)

            pe.wait_ge(w_split, -(-W1_AT // SPLIT_STEP))
            pe.wait_ge(hs_saved, STEPS + 2)
            project_v(0, range(2))
            project_qk(0, 1)
            project_v(0, range(2, 3))
            score(0, 0)
            project_v(0, range(3, 4))
            project_qk(1, 0)
            score(0, 1)
            project_qk(1, 1)
            pe.wait_ge(w_split, SPLITS)
            with pe.Fori(0, GROUPS - 2) as g:
                group(g)
            group(GROUPS - 2, projections=False)
            group(GROUPS - 1, scores=False, projections=False)

            def turn_residual(m):
                for tile in range(TILES):
                    a, b = divmod(tile % TILES_H * DIM + m * P, 512)
                    mm = pe.matmul((ps_s, ps_o)[tile // TILES_H][:, a, b:b + P], x2[:, m, tile * TILE_B:(tile + 1) * TILE_B, :],
                                   ident, start=True, stop=True)
                return mm

            def convolve(m):
                pe.wait_ge(x_split, m + 1)
                for d in range(STEPS):
                    w = conv_bd[:, m * STEPS + d].rearrange("p c t n -> p (c t) n")
                    cols = slice(d * BATCH, (d + 1) * BATCH)
                    a, b = divmod(d * BATCH, 512)
                    mm = three(ps_qk[:, 2 * m + a, b:b + BATCH], w[:, :, 0], w[:, :, 1],
                               xc_hi[:, m, cols], xc_lo[:, m, cols], True, True)
                mm.then_inc(convolved, 1)

            def expand(n, e):
                for i, at in enumerate((W1_AT, W2_AT)):
                    for k in range(KC):
                        a = at + (e * KC + k) * FF
                        mm = three(ps_s[:, e % 2, i * QT:(i + 1) * QT], w_hi[:, a:a + FF], w_lo[:, a:a + FF],
                                   y_hi[:, k, bass.ds(n * QT, QT)], y_lo[:, k, bass.ds(n * QT, QT)], k == 0, k == KC - 1)
                mm.then_inc(expanded, 1)

            def contract(e):
                a = W3_AT + e * DIM
                for q in range(QTILES):
                    mm = three(ps_o[:, e % 2, q * DIM:(q + 1) * DIM],
                               hid_hi[:, e % 2, q * P:(q + 1) * P], hid_lo[:, e % 2, q * P:(q + 1) * P],
                               w_hi[:, a:a + DIM], w_lo[:, a:a + DIM], True, True)
                mm.then_inc(contracted, 1)

            pe.wait_ge(consts_loaded, 48)
            pe.wait_ge(x2_updated, 4 * GROUPS + 2)
            turn_residual(0)
            pe.wait_ge(conv_bd_act, 1)
            pe.wait_ge(conv_bd_dve, CB - 2)
            pe.wait_ge(conv_bd_pool, 1)
            convolve(0)
            pe.wait_ge(x2_updated, 4 * GROUPS + 4)
            turn_residual(1).then_inc(residual_turned, 1)
            convolve(1)
            pe.wait_ge(y_turned, 2)
            keep_clock(KEEP_C, ps_qk[:, 1, :])

            def route_tokens():
                pe.wait_ge(y_split, 2 * KC)
                for tile in range(TILES):
                    for k in range(KC):
                        a = RW_AT + k * EXPERTS
                        mm = three(ps_qk[:, 0, tile * EXPERTS:(tile + 1) * EXPERTS],
                                   y_hi[:, k, tile * P:(tile + 1) * P], y_lo[:, k, tile * P:(tile + 1) * P],
                                   w_hi[:, a:a + EXPERTS], w_lo[:, a:a + EXPERTS], k == 0, k == KC - 1)
                mm.then_inc(routed, 1)

            def experts(n, first=False):
                for e in range(EXPERTS):
                    if not (first and e < 2):
                        pe.wait_ge(hidden_ready, n * EXPERTS + (e - 1))
                    if first and e == 0:
                        pe.wait_ge(residual_ready, 1)
                        pe.wait_ge(y_split, 2 * KC - 1)
                    expand(n, e)
                    if first and e == 0:
                        route_tokens()
                        pe.wait_ge(residual_ready, 2)
                    if not (first and e < 2):
                        pe.wait_ge(hidden_split, n * EXPERTS + (e - 1))
                        if not (first and e < 4):
                            pe.wait_ge(combined, n * EXPERTS + (e - 3))
                        contract((e - 2) % EXPERTS)

            experts(0, first=True)
            with pe.Fori(1, QUARTERS) as n:
                experts(n)
            for e in range(EXPERTS - 2, EXPERTS):
                at = (QUARTERS - 1) * EXPERTS + e
                pe.wait_ge(hidden_split, at + 1)
                pe.wait_ge(combined, at - 1)
                contract(e)

        @block.scalar
        def _(act):
            act.dma_start(bias_raw[:, :, :], gate_bias).then_inc(bias_loaded, 16)
            nc.scalar.preload_act_table(ACT.Exp)
            act.wait_ge(gru_loaded, 64)
            for u in range(2):
                nc.scalar.copy(x_now[:, u, :, :], xT[:, :, u, :]).then_inc(x_ready, 1)
            def gru_steps(i, split):
                for u in range(2):
                    t = i * 2 + u
                    act.wait_ge(reset_gates, t + 1)
                    nc.scalar.activation(reset[:, :], ps_o[:, u, CW:2 * CW], ACT.Tanh, scale=0.5).then_inc(reset_ready, 1)
                    act.wait_ge(update_gates, t + 1)
                    nc.scalar.activation(update[:, :], ps_s[:, u, 0:CW], ACT.Tanh, scale=0.5).then_inc(update_ready, 1)
                    act.wait_ge(cand_summed, t + 1)
                    nc.scalar.activation(cand[:, 1, :], ps_o[:, u, 3 * CW:4 * CW], ACT.Tanh).then_inc(cand_ready, 1)
                    act.wait_ge(hs_saved, t + 2)
                    act.wait_ge(x_projected, t + 1)
                    nc.scalar.copy(x_now[:, u, :, :], xT[:, :, bass.ds(t + 2, 1), :].rearrange("p k o b -> p k (o b)"))\
                        .then_inc(x_ready, 1)
                if split:
                    cols = bass.ds((i - A_SPLIT) * SPLIT_STEP, SPLIT_STEP)
                    nc.scalar.activation(w_hi[:, cols], arena[:, cols], ACT.Copy, scale=SPLIT).then_inc(w_headed, 1)

            with act.Fori(0, A_SPLIT) as i:
                gru_steps(i, False)
            act.wait_ge(x_loaded, 16)
            act.wait_ge(first_loaded[0], 16)
            with act.Fori(A_SPLIT, A_SPLIT_2) as i:
                gru_steps(i, True)
            act.wait_ge(first_loaded[1], 16)
            with act.Fori(A_SPLIT_2, A_SPLIT_END) as i:
                gru_steps(i, True)
            with act.Fori(A_SPLIT_END, A_LOOPS) as i:
                gru_steps(i, False)

            act.wait_ge(consts_loaded, 48)
            for m in range(KC):
                nc.scalar.activation(x2[:, m, :, :], xT[:, m, 0:STEPS, :].rearrange("p t b -> p b t"), ACT.Identity,
                                     bias=bo_s[:, m:m + 1]).then_inc(x2_updated, 2)

            def spread_k(j, half, heads):
                act.wait_ge(qk_rotated, j * 4 + (2 * half + 1))
                for h in heads:
                    rows = slice(HALF * h, HALF * (h + 1))
                    last = nc.scalar.copy(k_bd[rows, :, half * BH:(half + 1) * BH, h, :],
                                          k_s[rows, :, half * BH:(half + 1) * BH, :])
                if h == PER_GROUP - 1:
                    last.then_inc(k_spread, 1)

            def exponent(g, half):
                act.wait_ge(shifted, g * 2 + (half + 1))
                nc.scalar.activation(prob[:, half, :, :], soft[:, half, :, :], ACT.Exp).then_inc(exp_ready, 1)

            def head_o(g, n):
                act.wait_ge(attended, g * 4 + (n + 1))
                half, hp = n // 2, n % 2
                nc.scalar.copy(o_hi[:, hp, half * TH:(half + 1) * TH], ps_o[:, hp, :]).then_inc(o_headed, 1)

            def take_v(j, pairs=range(TILES // 2)):
                for n in pairs:
                    act.wait_ge(v_projected, j * 4 + (n + 1))
                    nc.scalar.copy(v_s[:, 2 * n:2 * n + 2, :], ps_o[:, n % 2, :]).then_inc(v_ready, 1)

            def take_q(half):
                act.wait_ge(qk_projected, 4 + 2 * half + 2)
                nc.scalar.copy(q_raw.rearrange("p a b t -> p (a b t)"), ps_qk[:, 2:4, :].rearrange("p a c -> p (a c)"))\
                    .then_inc(q_taken, 1)

            early, late = range(PER_GROUP // 2), range(PER_GROUP // 2, PER_GROUP)

            def group(g, scores=True, projections=True):
                head_o(g, 0)
                head_o(g, 1)
                if scores:
                    spread_k(g + 1, 1, early)
                head_o(g, 2)
                head_o(g, 3)
                if scores:
                    exponent(g + 1, 0)
                    spread_k(g + 1, 1, late)
                    if projections:
                        exponent(g + 1, 1)
                        take_v(g + 1)
                    else:
                        take_v(g + 1, range(2))
                        exponent(g + 1, 1)
                        take_v(g + 1, range(2, 4))
                if projections:
                    spread_k(g + 2, 0, range(PER_GROUP))

            act.wait_ge(k_diag_zeroed, 2)
            take_v(0, range(2))
            spread_k(0, 0, range(PER_GROUP))
            take_v(0, range(2, 4))
            spread_k(0, 1, range(PER_GROUP))
            exponent(0, 0)
            take_q(0)
            spread_k(1, 0, range(PER_GROUP))
            exponent(0, 1)
            act.wait_ge(q_multiplied, 1)
            take_q(1)
            with act.Fori(0, GROUPS - 2) as g:
                group(g)
            group(GROUPS - 2, projections=False)
            group(GROUPS - 1, scores=False, projections=False)

            nc.scalar.preload_act_table(ACT.Silu)
            act.wait_ge(conv_w_split, 1)
            rows = slice(STEPS * (CB - 1), P)
            nc.scalar.copy(conv_bd[rows, :, CB - 1], conv_w[rows, :, :, :]).then_inc(conv_bd_act, 1)
            for m in range(KC):
                act.wait_ge(x_turned, m + 1)
                nc.scalar.copy(xc_hi[:, m, :].rearrange("p (c b) -> p b c", b=BATCH), x_turned_f[:, m]).then_inc(x_headed, 1)

            def head_y(m, half):
                seqs = slice(half * BH, (half + 1) * BH)
                act.wait_ge(y_turned, 2 * m + half + 1)
                nc.scalar.activation(y_hi[:, m, half * TH:(half + 1) * TH], y_turned_f[:, m, seqs, :].rearrange("p b t -> p (b t)"),
                                     ACT.Identity, bias=conv_bs[:, m:m + 1]).then_inc(y_headed, 1)

            def take_residual(half):
                act.wait_ge(residual_turned, 1)
                bank = (ps_s, ps_o)[half]
                nc.scalar.copy(out_f[:, half * TILES_H:(half + 1) * TILES_H, :].rearrange("p n c -> p (n c)"),
                               bank[:, :, :].rearrange("p a c -> p (a c)")).then_inc(residual_ready, 1)

            head_y(0, 0)
            head_y(0, 1)
            take_residual(0)
            head_y(1, 0)
            head_y(1, 1)
            take_residual(1)

            def silu(n, e, first):
                act.wait_ge(expanded, n * EXPERTS + (e + 1))
                if not (first and e < 2):
                    act.wait_ge(hidden_ready, n * EXPERTS + (e - 1))
                nc.scalar.activation(gate_f[:, e % 2, :], ps_s[:, e % 2, 0:QT], ACT.Silu, scale=1.0 / SPLIT)\
                    .then_inc(silu_ready, 1)

            def head_hidden(n, e, first):
                act.wait_ge(hidden_ready, n * EXPERTS + (e + 1))
                if not (first and e < 2):
                    act.wait_ge(contracted, n * EXPERTS + (e - 1))
                nc.scalar.copy(hid_hi[:, e % 2, :], hid_f[:, e % 2, :]).then_inc(hidden_headed, 1)

            def quarter(n, first=False):
                for e in range(EXPERTS):
                    if first and e == 2:
                        act.wait_ge(margin_ready, 1)
                        nc.scalar.activation(route[:, :, 1:2], route[:, :, 0:1], ACT.Tanh, scale=0.5 / SPLIT)\
                            .then_inc(odds_ready, 1)
                    silu(n, e, first)
                    head_hidden(n, e, first)

            quarter(0, first=True)
            with act.Fori(1, QUARTERS) as n:
                quarter(n)

        @block.vector
        def _(dve):
            nc.vector.memset(warm[:, :], 0.0).then_inc(warm_ready, 1)
            nc.vector.memset(ones16[:, :], 0.0)
            dve.drain()
            for c in range(CB):
                rows = slice(BATCH * c, BATCH * (c + 1))
                last = nc.vector.memset(ones16[rows, rows], 1.0)
            last.then_inc(bias_ready, 1)
            dve.wait_ge(bias_loaded, 16)
            nc.vector.tensor_copy(bias16[:, :], bias_raw[:, 1, :]).then_inc(bias_ready, 1)
            dve.wait_ge(bias_ready, 2)
            nc.vector.tensor_tensor(bias_raw[:, 1, :], bias_raw[:, 1, :], bias16[:, :], ALU.subtract).then_inc(bias_ready, 1)
            dve.wait_ge(bias_ready, 3)
            nc.vector.tensor_tensor(bias16[:, :], bias_raw[:, 0, :], bias_raw[:, 1, :], ALU.add).then_inc(bias_ready, 1)
            dve.wait_ge(gru_loaded, 64)
            nc.vector.transpose(stateT[:, 1, :, :].rearrange("p e b -> p (e b)"), state[:, :]).then_inc(state_ready, 1)

            with dve.Fori(0, A_LOOPS) as i:
                for u in range(2):
                    t = i * 2 + u
                    dve.wait_ge(reset_ready, t + 1)
                    nc.vector.scalar_tensor_tensor(cand[:, 0, :], reset[:, :], 1.0, ps_o[:, u, 2 * CW:3 * CW], ALU.add, ALU.mult)\
                        .then_inc(reset_done, 1)
                    dve.wait_ge(reset_done, t + 1)
                    nc.vector.scalar_tensor_tensor(ps_o[:, u, 3 * CW:4 * CW], cand[:, 0, :], 0.5, ps_o[:, u, 0:CW],
                                                   ALU.mult, ALU.add).then_inc(cand_summed, 1)
                    dve.wait_ge(update_ready, t + 1)
                    nc.vector.tensor_scalar(blend[:, 1, :], update[:, :], -0.5, 0.5, ALU.mult, ALU.add).then_inc(blend_ready, 1)
                    dve.wait_ge(blend_ready, t * 3 + 1)
                    nc.vector.scalar_tensor_tensor(blend[:, 0, :], update[:, :], 1.0, state[:, :], ALU.add, ALU.mult)\
                        .then_inc(blend_ready, 1)
                    dve.wait_ge(cand_ready, t + 1)
                    nc.vector.tensor_tensor(blend[:, 2, :], cand[:, 1, :], blend[:, 1, :], ALU.mult).then_inc(blend_ready, 1)
                    dve.wait_ge(blend_ready, t * 3 + 3)
                    nc.vector.scalar_tensor_tensor(state[:, :], blend[:, 0, :], 0.5, blend[:, 2, :], ALU.mult, ALU.add)\
                        .then_inc(state_new, 1)
                    dve.wait_ge(state_new, t + 1)
                    nc.vector.transpose(stateT[:, u, :, :].rearrange("p e b -> p (e b)"), state[:, :]).then_inc(state_ready, 1)

            def rotate(j, half, pair):
                n = 2 * half + pair
                dve.wait_ge(qk_projected, j * 4 + (n + 1))
                if isinstance(j, int) and j == 0:
                    if n >= 2:
                        dve.wait_ge(qk_rotated, n - 1)
                else:
                    dve.wait_ge(qk_rotated, j * 4 + (n - 1))
                cos, sin, neg = rot[3 * pair:3 * pair + 3]
                src = ps_qk[:, 2 * pair:2 * pair + 2, :].rearrange("p a (b t) -> p a b t", b=BH)
                into = prods[:, pair, :, :].rearrange("p n (a b t) -> p n a b t", a=2, b=BH)
                nc.vector.tensor_tensor(into[:, 0].rearrange("p a b t -> p (a b) t"), src.rearrange("p a b t -> p (a b) t"),
                                        over(cos, 2 * BH), ALU.mult)
                nc.vector.tensor_tensor(into[:, 1, 0], src[:, 1], over(neg, BH), ALU.mult)
                nc.vector.tensor_tensor(into[:, 1, 1], src[:, 0], over(sin, BH), ALU.mult)\
                    .then_inc(qk_products, 2 if isinstance(j, int) and j == 1 else 1)

            rows = TILES_H * PER_GROUP

            def wide(a, half):
                return stats[:, half, a, :].rearrange("p (r o) -> p r o", o=1).broadcast_to([P, rows, STEPS])

            def softmax_front(g, half):
                dve.wait_ge(scored, g * 2 + (half + 1))
                nc.vector.tensor_tensor(soft[:, half, :, :], ps_s[:, half, :].rearrange("p (r t) -> p r t", t=STEPS),
                                        over(mask, rows), ALU.add).then_inc(masked, 1)
                dve.wait_ge(masked, g * 2 + (half + 1))
                nc.vector.tensor_reduce(stats[:, half, 0, :], soft[:, half, :, :], AX.X, ALU.max).then_inc(max_ready, 1)
                dve.wait_ge(max_ready, g * 2 + (half + 1))
                nc.vector.tensor_tensor(soft[:, half, :, :], soft[:, half, :, :], wide(0, half), ALU.subtract)\
                    .then_inc(shifted, 1)

            dve.wait_ge(pool_set, 1)

            def normalize(g, half):
                dve.wait_ge(exp_ready, g * 2 + (half + 1))
                nc.vector.tensor_reduce(stats[:, half, 1, :], prob[:, half, :, :], AX.X, ALU.add).then_inc(sum_ready, 1)
                dve.wait_ge(sum_ready, g * 2 + (half + 1))
                nc.vector.reciprocal(stats[:, half, 2, :], stats[:, half, 1, :]).then_inc(rsum_ready, 1)
                dve.wait_ge(rsum_ready, g * 2 + (half + 1))
                nc.vector.tensor_tensor(soft[:, half, :, :], prob[:, half, :, :], wide(2, half), ALU.mult)\
                    .then_inc(prob_ready, 1)

            def turn_probs(g, half):
                dve.wait_ge(prob_ready, g * 2 + (half + 1))
                for b in range(TILE_B):
                    part = slice(STEPS * b, STEPS * (b + 1))
                    last = nc.vector.transpose(p_bd[part, half, :, STEPS * b:STEPS * (b + 1)], soft[part, half, :, :])
                last.then_inc(prob_turned, 1)

            def softmax_back(g, half):
                normalize(g, half)
                turn_probs(g, half)

            def tail_o(g, n):
                half, hp = n // 2, n % 2
                dve.wait_ge(o_headed, g * 4 + (n + 1))
                cols = slice(half * TH, (half + 1) * TH)
                nc.vector.tensor_tensor(o_lo[:, hp, cols], ps_o[:, hp, :], o_hi[:, hp, cols], ALU.subtract)\
                    .then_inc(o_split, 1)

            def add_o(g, n, order):
                half, m = order[n]
                dve.wait_ge(o_projected, g * 4 + (n + 1))
                part = x2[:, m, half * BH:(half + 1) * BH, :].rearrange("p b t -> p (b t)")
                nc.vector.scalar_tensor_tensor(part, ps_qk[:, 2 * m + half, :], 1.0 / (SPLIT * SPLIT), part,
                                               ALU.mult, ALU.add).then_inc(x2_updated, 1)

            def spread_conv(c):
                dve.wait_ge(conv_w_split, 1)
                rows = slice(STEPS * c, STEPS * (c + 1))
                nc.vector.tensor_copy(conv_bd[rows, :, c], conv_w[rows, :, :, :]).then_inc(conv_bd_dve, 1)

            def group(g, scores=True, projections=True):
                tail_o(g, 0)
                tail_o(g, 1)
                if scores:
                    softmax_front(g + 1, 0)
                tail_o(g, 2)
                tail_o(g, 3)
                if not scores:
                    spread_conv(1)
                    return
                normalize(g + 1, 0)
                dve.wait_ge(x2_updated, g * 4 + 4)
                add_o(g, 0, HALF_FIRST)
                turn_probs(g + 1, 0)
                for n in range(1, 4):
                    add_o(g, n, HALF_FIRST)
                softmax_front(g + 1, 1)
                if not projections:
                    spread_conv(0)
                if projections:
                    rotate(g + 2, 0, 0)
                    rotate(g + 2, 0, 1)
                softmax_back(g + 1, 1)
                if projections:
                    rotate(g + 2, 1, 0)
                    rotate(g + 2, 1, 1)

            dve.wait_ge(consts_loaded, 48)
            dve.wait_ge(w_split, SPLITS)
            for half in range(2):
                for pair in range(2):
                    rotate(0, half, pair)
            softmax_front(0, 0)
            rotate(1, 0, 0)
            softmax_back(0, 0)
            softmax_front(0, 1)
            rotate(1, 1, 0)
            softmax_back(0, 1)
            with dve.Fori(0, GROUPS - 2) as g:
                group(g)
            group(GROUPS - 2, projections=False)
            group(GROUPS - 1, scores=False, projections=False)

            def turn_x(m):
                dve.wait_ge(x2_updated, 4 * GROUPS + 2 * (m + 1))
                nc.vector.transpose(x_turned_f[:, m].rearrange("p b c -> p (b c)"), x2[:, m, :, :].rearrange("p b t -> p (b t)"))\
                    .then_inc(x_turned, 1)

            def tail_x(m):
                dve.wait_ge(x_headed, m + 1)
                nc.vector.tensor_tensor(xc_lo[:, m, :].rearrange("p (c b) -> p b c", b=BATCH), x_turned_f[:, m],
                                        xc_hi[:, m, :].rearrange("p (c b) -> p b c", b=BATCH), ALU.subtract)\
                    .then_inc(x_split, 1)

            def turn_y(m, half):
                seqs = slice(half * BH, (half + 1) * BH)
                dve.wait_ge(convolved, m + 1)
                nc.vector.transpose(y_turned_f[:, m, seqs, :],
                                    ps_qk[:, 2 * m:2 * m + 2, :].rearrange("p a (c b) -> p b (a c)", b=BATCH)[:, seqs, :])\
                    .then_inc(y_turned, 1)

            def tail_y(m, half):
                cols = slice(half * TH, (half + 1) * TH)
                seqs = slice(half * BH, (half + 1) * BH)
                dve.wait_ge(y_headed, 2 * m + half + 1)
                nc.vector.scalar_tensor_tensor(y_lo[:, m, cols], y_turned_f[:, m, seqs, :].rearrange("p b t -> p (b t)"),
                                               conv_bs[:, m:m + 1], y_hi[:, m, cols], ALU.add, ALU.subtract).then_inc(y_split, 1)

            dve.wait_ge(x2_updated, 4 * GROUPS)
            add_o(GROUPS - 1, 0, CHUNK_FIRST)
            add_o(GROUPS - 1, 1, CHUNK_FIRST)
            turn_x(0)
            add_o(GROUPS - 1, 2, CHUNK_FIRST)
            add_o(GROUPS - 1, 3, CHUNK_FIRST)
            tail_x(0)
            turn_x(1)
            tail_x(1)
            turn_y(0, 0)
            turn_y(0, 1)
            tail_y(0, 0)
            tail_y(0, 1)
            turn_y(1, 0)
            turn_y(1, 1)
            tail_y(1, 0)
            tail_y(1, 1)

            def find_top():
                dve.wait_ge(routed, 1)
                nc.vector.tensor_copy(logits[:, :, :], ps_qk[:, 0, 0:TILES * EXPERTS].rearrange("p (q e) -> p q e", q=TILES))
                dve.drain()
                for q in range(TILES):
                    nc.vector.max(top[:, q, :], logits[:, q, :])
                dve.drain()
                nc.vector.tensor_tensor(route[:, :, 0:1], top[:, :, 0:1], top[:, :, 1:2], ALU.subtract)\
                    .then_inc(margin_ready, 1)
                for q in range(TILES):
                    nc.vector.max_index(top_at[:, q, :], top[:, q, :], logits[:, q, :]).then_inc(top_found, 1)
                dve.wait_ge(top_found, TILES)
                nc.vector.tensor_copy(top_f[:, :, :], top_at[:, :, :]).then_inc(top_cast, 1)

            def choose():
                dve.wait_ge(odds_ready, 1)
                nc.vector.tensor_scalar(route[:, :, 2:3], route[:, :, 1:2], 0.5 / SPLIT, 0.5 / SPLIT, ALU.mult, ALU.add)
                nc.vector.tensor_scalar(route[:, :, 3:4], route[:, :, 1:2], -0.5 / SPLIT, 0.5 / SPLIT, ALU.mult, ALU.add)\
                    .then_inc(shares_ready, 1)
                dve.wait_ge(top_cast, 1)

                def every_expert(a):
                    return a.rearrange("p q (s o) -> p q s o", o=1).broadcast_to([P, TILES, 2, EXPERTS])

                nc.vector.tensor_tensor(pick[:, :, 0:2, :], every_expert(top_f[:, :, 0:2]),
                                        iota.rearrange("p (q s e) -> p q s e", q=1, s=1).broadcast_to([P, TILES, 2, EXPERTS]),
                                        ALU.is_equal).then_inc(places_found, 1)
                dve.wait_ge(places_found, 1)
                dve.wait_ge(shares_ready, 1)
                nc.vector.tensor_tensor(pick[:, :, 0:2, :], pick[:, :, 0:2, :], every_expert(route[:, :, 2:4]), ALU.mult)\
                    .then_inc(picks_ready, 1)
                dve.wait_ge(picks_ready, 1)
                nc.vector.tensor_tensor(pick[:, :, 2, :], pick[:, :, 0, :], pick[:, :, 1, :], ALU.add).then_inc(gates_summed, 1)
                dve.wait_ge(gates_summed, 1)
                dve.wait_ge(residual_ready, 2)

            def hidden(n, e, first):
                dve.wait_ge(silu_ready, n * EXPERTS + (e + 1))
                if not (first and e < 2):
                    dve.wait_ge(hidden_split, n * EXPERTS + (e - 1))
                nc.vector.scalar_tensor_tensor(hid_f[:, e % 2, :], ps_s[:, e % 2, QT:2 * QT], 1.0 / SPLIT,
                                               gate_f[:, e % 2, :], ALU.mult, ALU.mult).then_inc(hidden_ready, 1)

            def tail_hidden(n, e):
                dve.wait_ge(hidden_headed, n * EXPERTS + (e + 1))
                nc.vector.tensor_tensor(hid_lo[:, e % 2, :], hid_f[:, e % 2, :], hid_hi[:, e % 2, :], ALU.subtract)\
                    .then_inc(hidden_split, 1)

            def combine(n, e, contracted_by, first):
                dve.wait_ge(contracted, contracted_by)
                if not (first and e == 0):
                    dve.wait_ge(combined, contracted_by - 1)
                for q in range(QTILES):
                    tile = bass.ds(n * QTILES + q, 1)
                    row = out_f[:, tile, :].rearrange("p o c -> p (o c)")
                    last = nc.vector.scalar_tensor_tensor(row, ps_o[:, e % 2, q * DIM:(q + 1) * DIM],
                                                          pick[:, tile, 2, e:e + 1].rearrange("p o c -> p (o c)"), row,
                                                          ALU.mult, ALU.add)
                last.then_inc(combined, 1)

            def quarter(n, first=False):
                for e in range(EXPERTS):
                    hidden(n, e, first)
                    if first and e == 2:
                        choose()
                    if e >= 2:
                        combine(n, e - 2, n * EXPERTS + (e - 1), first)
                    elif not first:
                        combine(n - 1, EXPERTS + e - 2, n * EXPERTS + (e - 1), False)
                    tail_hidden(n, e)
                    if first and e == 0:
                        find_top()

            quarter(0, first=True)
            with dve.Fori(1, QUARTERS) as n:
                quarter(n)
            for e in range(EXPERTS - 2, EXPERTS):
                combine(QUARTERS - 1, e, (QUARTERS - 1) * EXPERTS + (e + 1), False)

        @block.gpsimd
        def _(pool):
            nc.gpsimd.memset(split_by[:, :], SPLIT).then_inc(hs_saved, 2)
            nc.gpsimd.memset(xT[:, :, STEPS:STEPS + 2, :], 0.0).then_inc(o_w_ready, 1)
            nc.gpsimd.memset(p_bd[:, :, :, :], 0.0).then_inc(pool_set, 1)
            for part in range(2):
                nc.gpsimd.memset(k_bd[:, part, :, :, :], 0.0).then_inc(k_diag_zeroed, 1)
            pool.wait_ge(k_diag_zeroed, 2)
            def split_state(t, u):
                now = bass.ds(t, 1)
                pool.wait_ge(state_ready, t + 2)
                hi = hs_hi[:, :, :, now].rearrange("p k b o -> p k (b o)")
                lo = hs_lo[:, :, :, now].rearrange("p k b o -> p k (b o)")
                nc.gpsimd.tensor_copy(hi, stateT[:, u, :, :]).then_inc(hs_hi_saved, 1)
                pool.wait_ge(hs_hi_saved, t + 1)
                nc.gpsimd.tensor_tensor(lo, stateT[:, u, :, :], hi, ALU.subtract).then_inc(hs_saved, 1)

            with pool.Fori(0, A_SPLIT + 1) as i:
                for u in range(2):
                    split_state(i * 2 + u, u)
            with pool.Fori(A_SPLIT + 1, A_SPLIT_END + 1) as i:
                cols = bass.ds((i - (A_SPLIT + 1)) * SPLIT_STEP, SPLIT_STEP)
                split_state(i * 2, 0)
                pool.wait_ge(w_headed, i - A_SPLIT)
                nc.gpsimd.tensor_tensor(arena[:, cols], arena[:, cols], split_by[:, 0:1].broadcast_to([P, SPLIT_STEP]), ALU.mult)\
                    .then_inc(w_scaled, 1)
                split_state(i * 2 + 1, 1)
                pool.wait_ge(w_scaled, i - A_SPLIT)
                nc.gpsimd.tensor_tensor(w_lo[:, cols], arena[:, cols], w_hi[:, cols], ALU.subtract).then_inc(w_split, 1)
            with pool.Fori(A_SPLIT_END + 1, A_LOOPS) as i:
                for u in range(2):
                    split_state(i * 2 + u, u)

            def add_products(j, half, pair):
                n = 2 * half + pair
                pool.wait_ge(qk_products, j * 4 + (n + 1))
                into = (k_s, q_s)[pair][:, :, half * BH:(half + 1) * BH, :].rearrange("p a b t -> p a (b t)")
                both = prods[:, pair, :, :].rearrange("p n (a c) -> p n a c", a=2)
                nc.gpsimd.tensor_tensor(into, both[:, 0], both[:, 1], ALU.add).then_inc(qk_rotated, 1)

            def split_weights(raw, at, order, ready):
                cols = raw.shape[1]
                head, tail = w_hi[:, at:at + cols], w_lo[:, at:at + cols]
                by = split_by[:, 0:1].broadcast_to([P, cols])
                nc.gpsimd.tensor_tensor(head, raw[:, :], by, ALU.mult).then_inc(w_headed, 1)
                pool.wait_ge(w_headed, order)
                nc.gpsimd.tensor_tensor(raw[:, :], raw[:, :], by, ALU.mult).then_inc(w_scaled, 1)
                pool.wait_ge(w_scaled, order)
                nc.gpsimd.tensor_tensor(tail, raw[:, :], head, ALU.subtract).then_inc(ready, 1)

            def products(j, half):
                for pair in range(2):
                    add_products(j, half, pair)

            def multiply_q(half):
                pool.wait_ge(q_taken, half + 1)
                pool.wait_ge(qk_rotated, 4 + 2 * half)
                cos, sin, neg = rot[3:6]
                into = prods[:, 1, :, :].rearrange("p n (a b t) -> p n a b t", a=2, b=BH)
                nc.gpsimd.tensor_tensor(into[:, 0].rearrange("p a b t -> p (a b) t"), q_raw.rearrange("p a b t -> p (a b) t"),
                                        over(cos, 2 * BH), ALU.mult)
                nc.gpsimd.tensor_tensor(into[:, 1, 0], q_raw[:, 1], over(neg, BH), ALU.mult)
                nc.gpsimd.tensor_tensor(into[:, 1, 1], q_raw[:, 0], over(sin, BH), ALU.mult).then_inc(q_multiplied, 1)

            def split_qk(j, order):
                pool.wait_ge(qk_loaded, (j - 1) * 16)
                pool.wait_ge(qk_projected, 4 if isinstance(j, int) and j == 2 else j * 4)
                split_weights(raw_qk, QK_AT, order, qk_w_ready)

            def group(g, order, last=False, projections=True):
                pool.wait_ge(v_loaded, g * 16 + 16)
                pool.wait_ge(v_projected, g * 4 + 4)
                split_weights(raw_v, V_AT, order + 1, v_w_ready)
                if not projections:
                    pool.wait_ge(conv_w_headed, 1)
                    nc.gpsimd.tensor_tensor(conv_w[:, :, :, 1], conv_raw, conv_w[:, :, :, 0], ALU.subtract).then_inc(conv_w_split, 1)
                pool.wait_ge(o_loaded, g * 16 + 16)
                pool.wait_ge(o_projected, g * 4 + 4)
                split_weights(raw_o, WO_AT, order + 2, o_w_ready)
                if projections:
                    if last:
                        pool.wait_ge(conv_loaded, 16)
                        pool.wait_ge(x2_updated, 4)
                        nc.gpsimd.tensor_copy(conv_w[:, :, :, 0], conv_raw).then_inc(conv_w_headed, 1)
                    products(g + 2, 0)
                    products(g + 2, 1)
                if not last:
                    split_qk(g + 3, order + 3)

            products(0, 0)
            products(0, 1)
            split_qk(2, SPLITS + 1)
            add_products(1, 0, 0)
            multiply_q(0)
            pool.wait_ge(q_multiplied, 1)
            add_products(1, 0, 1)
            add_products(1, 1, 0)
            multiply_q(1)
            pool.wait_ge(q_multiplied, 2)
            add_products(1, 1, 1)
            with pool.Fori(0, GROUPS - 3) as g:
                group(g, g * 3 + (SPLITS + 1))
            group(GROUPS - 3, 3 * (GROUPS - 3) + SPLITS + 1, last=True)
            group(GROUPS - 2, 3 * (GROUPS - 2) + SPLITS, last=True, projections=False)
            pool.wait_ge(conv_w_split, 1)
            pool.wait_ge(o_w_ready, GROUPS)
            pool.wait_ge(scored, 2 * GROUPS)
            rows = slice(2 * STEPS, 3 * STEPS)
            nc.gpsimd.tensor_copy(conv_bd[rows, :, 2], conv_w[rows, :, :, :]).then_inc(conv_bd_pool, 1)


def _tables(np):
    inv = (1.0 / 10000.0 ** (np.arange(0, HEAD_DIM, 2, dtype=np.float32) / np.float32(HEAD_DIM))).astype(np.float32)
    angle = (np.arange(STEPS, dtype=np.float32)[None, :] * inv[:, None]).astype(np.float32)
    cos, sin = np.cos(angle).astype(np.float32), np.sin(angle).astype(np.float32)
    t = np.zeros((P, TAB_COLS), np.float32)
    for pair, scale in enumerate((1.0 / SPLIT, HEAD_DIM ** -0.5 / SPLIT)):
        for n, table in enumerate((cos, sin, -sin)):
            at = (3 * pair + n) * STEPS
            t[:, at:at + STEPS] = np.tile(table * np.float32(scale), (P // HALF, 1))
    q, k = np.arange(P)[:, None] % STEPS, np.arange(STEPS)[None, :]
    t[:, TAB_MASK:TAB_MASK + STEPS] = np.where(q >= k, 0.0, -1e30)
    t[:, TAB_IDENT:TAB_IDENT + P] = np.eye(P)
    t[:, TAB_IOTA:] = np.arange(EXPERTS)
    return t


def kernel(**inputs):
    import numpy as np
    import concourse.bacc as _bacc
    from concourse.bass_utils import run_bass_kernel_spmd as _run

    a = {n: np.asarray(v) for n, v in inputs.items()}
    con = np.ascontiguousarray

    x_t = con(a["x"].transpose(2, 1, 0).reshape(KC, P, STEPS, BATCH).transpose(1, 0, 2, 3))
    h0 = con(a["cond_2048"].reshape(BATCH, CB, CW).transpose(1, 0, 2).reshape(P, CW))
    w_ih = con(a["L0_cond_W_ih"].reshape(KC, P, 3, CB, CW).transpose(1, 0, 3, 2, 4)[:, :, :, [2, 0, 1]]
               .reshape(P, KC, CB, 3 * CW))

    def state_rows(w):
        return w.reshape(CB, KC, 32, -1).transpose(0, 2, 1, 3).reshape(P, KC, -1)

    w_hh = con(state_rows(a["L0_cond_W_hh"]).reshape(P, KC, 3, CB, CW).transpose(0, 1, 3, 2, 4)[:, :, :, [0, 2, 1]]
               .reshape(P, KC, CB, 3 * CW))
    bi, bh = (a[n].reshape(3, CB, CW) for n in ("L0_cond_b_ih", "L0_cond_b_hh"))
    biases = np.zeros((CB, 2, 4 * CW), np.float32)
    for n, g in ((0, 2), (1, 0), (3, 1)):
        biases[:, 0, n * CW:(n + 1) * CW] = bi[g]
    for n, g in ((1, 0), (2, 2), (3, 1)):
        biases[:, 1, n * CW:(n + 1) * CW] = bh[g]
    gate_bias = np.zeros((CB, BATCH, 2, 4 * CW), np.float32)
    for plane in range(2):
        gate_bias[:, 2 * plane:2 * plane + 2, plane] = biases
    gate_bias = gate_bias.reshape(P, 2, 4 * CW)

    def rotary_rows(w):
        return w.reshape(GROUPS, PER_GROUP, 2, HALF, DIM).transpose(0, 2, 1, 3, 4).reshape(GROUPS, DIM, DIM)

    def row_chunks(w):
        return con(np.stack([state_rows(m.T) for m in w]).reshape(GROUPS, P, -1))

    w_qk = row_chunks(np.concatenate([rotary_rows(a["L0_attn_Wk"]), rotary_rows(a["L0_attn_Wq"])], 1))
    w_v = row_chunks(a["L0_attn_Wv"].reshape(GROUPS, VW, DIM))
    w_o = con(a["L0_attn_Wo"].T.reshape(GROUPS, HP, P, DIM).transpose(0, 2, 1, 3).reshape(GROUPS, P, WO_COLS))

    def up(w):
        return w.reshape(EXPERTS, KC, P, FF).transpose(2, 0, 1, 3).reshape(P, W1_COLS)

    w_first = con(np.concatenate([
        w_qk[0], w_qk[1], w_v[0], w_o[0], a["L0_ffn_router_w"].T.reshape(KC, P, EXPERTS).transpose(1, 0, 2).reshape(P, RW_COLS),
        up(a["L0_ffn_w1"]), up(a["L0_ffn_w2"]), a["L0_ffn_w3"].transpose(1, 0, 2).reshape(P, W3_COLS),
        np.zeros((P, SPLIT_COLS - USED_COLS), np.float32)], 1))
    padded = np.zeros((DIM, 2 * STEPS - 1), np.float32)
    padded[:, STEPS - 1:] = a["cond_2048"].T[:, ::-1]
    w_conv = np.stack([padded[:, STEPS - 1 - s:2 * STEPS - 1 - s] for s in range(STEPS)])
    w_conv = con(w_conv.reshape(STEPS, KC, CB, STEPS, STEPS).transpose(2, 0, 1, 3, 4).reshape(P, CH_GROUPS, STEPS))
    arrays = {
        "x_t": x_t, "h0": h0, "w_ih": w_ih, "w_hh": w_hh, "gate_bias": gate_bias, "w_first": w_first,
        "w_qk": con(w_qk[2:]), "w_v": con(w_v[1:]), "w_o": con(w_o[1:]),
        "bo": con(a["L0_attn_bo"].reshape(KC, P).T), "tables": _tables(np),
        "w_conv": w_conv,
        "conv_b": con(a["L0_cond2_b"].reshape(KC, P).T),
    }
    nc = _bacc.Bacc("TRN2", target_bir_lowering=False, num_devices=1)
    args = [nc.dram_tensor(f"{n}_dram", v.shape, mybir.dt.from_np(v.dtype), kind="ExternalInput").ap()
            for n, v in arrays.items()]
    out = nc.dram_tensor("out_dram", (QUARTERS, QTILES, P, DIM), F32, kind="ExternalOutput").ap()
    block_kernel(nc, *args, out)
    r = _run(nc, [{f"{n}_dram": v for n, v in arrays.items()}], core_ids=[0])
    return r.results[0]["out_dram"].reshape(BATCH, STEPS, DIM)
```
